# Optimizing a Trainium2 kernel written in Bass

```python
import numpy as np
import jax
import jax.numpy as jnp

def _softmax(x, axis=-1):
    return jax.nn.softmax(x, axis=axis)

def _gelu(x):
    return jax.nn.gelu(x, approximate=True)

def _silu(x):
    return jax.nn.silu(x)

def _sigmoid(x):
    return jax.nn.sigmoid(x)

def _layernorm(x, axis=-1, eps=1e-05):
    m = jnp.mean(x, axis=axis, keepdims=True)
    v = jnp.var(x, axis=axis, keepdims=True)
    return (x - m) / jnp.sqrt(v + eps)

def _scatter_add(tgt, idx, src, axis=0):
    return tgt.at[idx].add(src)

def _segment_sum(src, seg, n):
    return jax.ops.segment_sum(src, seg, n)
kernel_name = 'mk_prb_d1_jaxref_r4_4d53b1'

def setup_inputs(seed: int=0):
    np.random.seed(seed)
    _w = jnp.asarray

    def _L0_attn_setup():
        import jax, jax.numpy as jnp
        import numpy as np
        DECAY_CONSTANT = 1.0

        def _build_decay_matrices(weight, decay_value, S, dtype):
            i = jnp.arange(S)[:, None]
            j = jnp.arange(S)[None, :]
            mask = j >= i
            e = jnp.where(mask, (j - i).astype(dtype), jnp.asarray(0.0, dtype))
            dv0 = jnp.clip(decay_value[0, 0], 0.9, 1.0).astype(dtype)
            dv1 = jnp.clip(decay_value[1, 0], 0.9, 1.0).astype(dtype)
            w0 = weight[0].astype(dtype)
            w1 = weight[1].astype(dtype)
            Wr = jnp.where(mask, w0[:, None] * (dv0 ** e / DECAY_CONSTANT), jnp.asarray(0.0, dtype))
            Wc = jnp.where(mask, w1[None, :] * dv1 ** (e / DECAY_CONSTANT), jnp.asarray(0.0, dtype))
            return (Wr, Wc)
        key = jax.random.key(seed)
        kx, kw = jax.random.split(key)
        B, E, S = (4, 512, 512)
        x = jax.random.normal(kx, (B, E, S), dtype=jnp.float32)
        weight = jax.random.normal(kw, (2, S), dtype=jnp.float32)
        bias = jnp.zeros((S,), dtype=jnp.float32)
        decay_value = jnp.ones((2, 1), dtype=jnp.float32)
        return {'x': x, 'weight': weight, 'bias': bias, 'decay_value': decay_value}
    _L0_attn_in = _L0_attn_setup()

    def _L0_ffn_setup():
        import jax, jax.numpy as jnp
        import numpy as np
        E = 8
        TOP_K = 2
        D = 512
        M = 1792
        B, S = (2, 512)
        key = jax.random.key(seed)
        kx, kg, k1, k2, k3 = jax.random.split(key, 5)
        x = jax.random.normal(kx, (B, S, D), dtype=jnp.float32)
        gate_w = jax.random.normal(kg, (D, E), dtype=jnp.float32) / np.sqrt(D)
        w1 = jax.random.normal(k1, (E, D, M), dtype=jnp.float32) / np.sqrt(D)
        w2 = jax.random.normal(k2, (E, M, D), dtype=jnp.float32) / np.sqrt(M)
        w3 = jax.random.normal(k3, (E, D, M), dtype=jnp.float32) / np.sqrt(D)
        return {'x': x, 'gate_w': gate_w, 'w1': w1, 'w2': w2, 'w3': w3}
    _L0_ffn_in = _L0_ffn_setup()
    _d = {'L0_attn_x': _L0_attn_in['x'], 'L0_attn_weight': _L0_attn_in['weight'], 'L0_attn_bias': _L0_attn_in['bias'], 'L0_attn_decay_value': _L0_attn_in['decay_value'], 'L0_ffn_gate_w': _L0_ffn_in['gate_w'], 'L0_ffn_w1': _L0_ffn_in['w1'], 'L0_ffn_w2': _L0_ffn_in['w2'], 'L0_ffn_w3': _L0_ffn_in['w3']}
    _x0 = _d['L0_attn_x']
    _d['L0_attn_x'] = jax.random.normal(jax.random.fold_in(jax.random.key(seed), 1), (2, 1024, 512), dtype=_x0.dtype)
    del _x0
    return _d

def reference(L0_attn_x, L0_attn_weight, L0_attn_bias, L0_attn_decay_value, L0_ffn_gate_w, L0_ffn_w1, L0_ffn_w2, L0_ffn_w3):

    def _L0_attn_ref(x, weight, bias, decay_value):
        import jax, jax.numpy as jnp
        import numpy as np
        DECAY_CONSTANT = 1.0

        def _build_decay_matrices(weight, decay_value, S, dtype):
            i = jnp.arange(S)[:, None]
            j = jnp.arange(S)[None, :]
            mask = j >= i
            e = jnp.where(mask, (j - i).astype(dtype), jnp.asarray(0.0, dtype))
            dv0 = jnp.clip(decay_value[0, 0], 0.9, 1.0).astype(dtype)
            dv1 = jnp.clip(decay_value[1, 0], 0.9, 1.0).astype(dtype)
            w0 = weight[0].astype(dtype)
            w1 = weight[1].astype(dtype)
            Wr = jnp.where(mask, w0[:, None] * (dv0 ** e / DECAY_CONSTANT), jnp.asarray(0.0, dtype))
            Wc = jnp.where(mask, w1[None, :] * dv1 ** (e / DECAY_CONSTANT), jnp.asarray(0.0, dtype))
            return (Wr, Wc)
        B, E, S = x.shape
        Wr, Wc = _build_decay_matrices(weight, decay_value, S, x.dtype)
        out = jnp.einsum('bes,st->bet', x, Wr + Wc)
        out = out + bias.astype(x.dtype)
        return out

    def _L0_ffn_ref(x, gate_w, w1, w2, w3):
        import jax, jax.numpy as jnp
        import numpy as np
        E = 8
        TOP_K = 2
        D = 512
        M = 1792
        B, S = (2, 512)
        b, s, d = x.shape
        x_flat = x.reshape(-1, d)
        router_logits = x_flat @ gate_w
        router_probs = jax.nn.softmax(router_logits, axis=-1)
        topk_w, topk_idx = jax.lax.top_k(router_probs, TOP_K)
        topk_w = topk_w / jnp.sum(topk_w, axis=-1, keepdims=True)
        idx_flat = topk_idx.reshape(-1)
        sort_idx = jnp.argsort(idx_flat)
        x_rep_sort = jnp.take(x_flat, sort_idx // TOP_K, axis=0)
        group_sizes = jnp.bincount(idx_flat, length=E).astype(jnp.int32)
        h = jax.lax.ragged_dot(x_rep_sort, w1, group_sizes)
        h = jax.nn.silu(h) * jax.lax.ragged_dot(x_rep_sort, w3, group_sizes)
        out_sort = jax.lax.ragged_dot(h, w2, group_sizes)
        inv_sort_idx = jnp.argsort(sort_idx)
        out_rep = jnp.take(out_sort, inv_sort_idx, axis=0).reshape(-1, TOP_K, d)
        out = jnp.einsum('tkd,tk->td', out_rep, topk_w)
        return out.reshape(b, s, d)
    x = L0_attn_x
    xn = _layernorm(x, axis=-1)
    x = x + _L0_attn_ref(xn, L0_attn_weight, L0_attn_bias, L0_attn_decay_value) + _L0_ffn_ref(xn, L0_ffn_gate_w, L0_ffn_w1, L0_ffn_w2, L0_ffn_w3)
    return x

_drawn_inputs = setup_inputs


def setup_inputs(seed=0):
    import zlib

    import numpy as np

    out = dict(_drawn_inputs(seed))
    spreads = {'L0_attn_bias': (0.0, 0.289), 'L0_attn_decay_value': (1.0, 0.2)}
    factors = {}
    for name, (base, spread) in spreads.items():
        noise = np.random.default_rng([zlib.crc32(name.encode()), seed]).standard_normal(out[name].shape)
        drawn = base * np.exp(spread * noise) if base else spread * noise
        out[name] = jnp.asarray(drawn.astype(out[name].dtype))
    for name, factor in factors.items():
        out[name] = (out[name] * factor).astype(out[name].dtype)
    return out
```

```python
from contextlib import ExitStack

import concourse.bass as bass
from concourse import mybir

F32 = mybir.dt.float32
F32R = mybir.dt.float32r
I32 = mybir.dt.int32
U32 = mybir.dt.uint32
ALU = mybir.AluOpType
ACT = mybir.ActivationFunctionType
AX_X = mybir.AxisListType.X
ds = bass.ds

P = 128
TOP_K = 2
EPS = 1e-5
TPS = 5

RAW_BUF = [0, 1, 2, 0, 1, 2, 1]
W13_BUF = [0, 1, 2, 0, 1, 2, 3]
W2_BUF = [0, 1, 2, 0, 1, 2, 3]


def reuse_distance(bufs):
    n = len(bufs)
    return [next(d for d in range(1, n + 1) if bufs[(c - d) % n] == bufs[c]) for c in range(n)]


def decay_moe_kernel(nc, x, weight, bias, decay_value, gate_w, w1, w2, w3, out):
    B, S, D = x.shape
    T = B * S
    E, _, M = w1.shape
    NT = T // P
    DC = D // P
    MC = M // len(RAW_BUF)
    NCH = M // MC
    MP = MC // P
    SLOTS = TPS * P
    NS = (TOP_K * T + E * (SLOTS - 1)) // SLOTS
    NST = NS + 1
    NTAB = NST * TPS
    G = 4
    NG = NT // G
    NKT = TOP_K * NT
    MAX_SB = -(-T // SLOTS)
    W13 = DC * 2 * MC
    W2E = MP * D
    RAW_DIST, W2_DIST = map(reuse_distance, (RAW_BUF, W2_BUF))

    def w2_used(k):
        q, r = divmod(k, NCH)
        return q * (NCH - 1) + r + 1 if r < NCH - 1 else (q + 1) * (NCH - 1) + 1

    RAW_CREDIT = 1 + max(RAW_DIST[n % NCH] - n - 1 for n in range(2, NCH + 2))
    USED_CREDIT = 1 + max(-w2_used(n - W2_DIST[n % NCH]) for n in range(1, NCH + 1))
    DECAY_CREDIT = 2
    XN_CREDIT = 16
    G_CREDIT = 2
    GT_CREDIT = 1
    Y_CREDIT = 1

    xf = x.rearrange("b s d -> (b s) d")
    x_tiles = xf.rearrange("(g q p) d -> g p q d", p=P, q=G)
    out_tiles = out[0:T, :].rearrange("(g q p) d -> g p q d", p=P, q=G)
    xn_dram = nc.dram_tensor("xn_rows", (T + P, D), F32).ap()
    xn_tiles = xn_dram[0:T, :].rearrange("(t p) d -> t p d", p=P)

    ctx = ExitStack()
    with ctx:
        ctx.enter_context(nc.allow_non_contiguous_dma(reason="small vectors"))
        at = [nc.sbuf_base + (-nc.sbuf_base) % 64]

        def place(name, shape, dt, offset=None):
            size = 4
            for n in shape[1:]:
                size *= n
            if offset is None:
                offset = at[0]
                at[0] += size + (-size) % 64
            return nc.alloc_sbuf_tensor_at(name, shape, dt, offset=offset)

        raw = [place(f"w_raw{b}", [P, W13 + W2E], F32) for b in range(3)]
        w13_at, w13_hi, w13_lo = [], [], []
        for b in range(4):
            w13_at.append(at[0])
            w13_hi.append(place(f"w13_hi{b}", [P, W13], F32R))
            w13_lo.append(place(f"w13_lo{b}", [P, W13], F32R))
        w2_at = []
        w2_hi, w2_lo = [], []
        for b in range(4):
            w2_at.append(at[0])
            w2_hi.append(place(f"w2_hi{b}", [P, W2E], F32R))
            w2_lo.append(place(f"w2_lo{b}", [P, W2E], F32R))
        o = w2_at[1]
        power = [place(f"power{k}", [P, D], F32, o + 4 * D * k) for k in range(2)]
        w1_row = place("w1_row", [P, D], F32, o + 8 * D)
        bias_row = place("bias_row", [P, D], F32, o + 12 * D)
        decay = place("decay", [P, DC, D], F32, o + 16 * D)
        zeros = place("zeros", [P, D], F32, o + (16 + 4 * DC) * D)
        diagonal = place("diagonal", [P, D], F32, o + (20 + 4 * DC) * D)
        ones_row = place("ones_row", [P, D], F32, o + (24 + 4 * DC) * D)
        assert (28 + 4 * DC) * D <= at[0] - o
        x_at = at[0]
        xs = place("xs", [P, NT, D], F32)
        o = x_at
        silu, g, gT_hi, gT_lo, y = [], [], [], [], []
        for j in range(2):
            silu.append(place(f"silu{j}", [P, MC], F32, o)); o += 4 * MC
        for j in range(TPS):
            g.append(place(f"g{j}", [P, MC], F32, o)); o += 4 * MC
        for j in range(TPS):
            gT_hi.append(place(f"gT_hi{j}", [P, MP, P], F32R, o)); o += 4 * MC
            gT_lo.append(place(f"gT_lo{j}", [P, MP, P], F32R, o)); o += 4 * MC
        for j in range(TPS):
            y.append(place(f"y{j}", [P, D], F32, o)); o += 4 * D
        assert o <= x_at + 4 * NT * D
        xg = [place(f"x_rows{j}", [P, D], F32) for j in range(TPS)]
        xT_at = at[0]
        xT_hi = [place(f"xT_hi{j}", [P, DC, P], F32R) for j in range(TPS)]
        xT_lo = [place(f"xT_lo{j}", [P, DC, P], F32R) for j in range(TPS)]
        pick_tile = place("pick_tile", [P, NKT, 2, NTAB], F32, xT_at)
        xn_at = w13_at[3]
        xn = [place(f"xn{q}", [P, D], F32, xn_at + 4 * D * q) for q in range(G)]
        xnT = [place(f"xnT{q}", [P, DC, P], F32, xn_at + 4 * D * (G + q)) for q in range(G)]
        pick_lane = place("pick_lane", [P, NKT, P], F32, xn_at)

        ident = place("ident", [P, P], F32)
        before = place("before", [P, P], F32)
        ones = place("ones", [P, P], F32)
        lane_iota = place("lane_iota", [P, P], F32)
        scrap = place("scrap", [P, 16], F32)
        token1 = place("token1", [P, NT], F32)
        rev = place("rev", [P, E], F32)
        sb_iota = place("sb_iota", [P, NST], F32)
        spare = place("spare", [P, 1], F32)
        dv = place("dv", [P, 2], F32)
        w0_col = place("w0_col", [P, DC], F32)
        gate = place("gate", [P, DC, E], F32)
        stats = place("stats", [P, NT, 6], F32)
        mv = place("mv", [P, NT, 2], F32)
        ve = place("ve", [P, NT], F32)
        sd = place("sd", [P, NT], F32)
        rs = place("rs", [P, NT], F32)
        nt1 = place("nt1", [P, NT], F32)
        rstd = place("rstd", [P, NT], F32)
        R = [place(f"route{n}", [P, NT, E], F32) for n in range(8)]
        V = [place(f"route_v{n}", [P, NT], F32) for n in range(8)]
        C = [place(f"count{n}", [P, E], F32) for n in range(8)]
        Q = [place(f"sb_tab{n}", [P, NST, E], F32) for n in range(3)]
        slot_f = place("slot_f", [P, TOP_K, NT], F32)
        slot_i = place("slot_i", [P, TOP_K, NT], I32)
        lane_i = place("lane_i", [P, TOP_K, NT], I32)
        tile_i = place("tile_i", [P, TOP_K, NT], I32)
        lane_f = place("lane_f", [P, TOP_K, NT], F32)
        tile_f = place("tile_f", [P, TOP_K, NT], F32)
        top_w = place("top_w", [P, TOP_K, NT], F32)
        tab_f = place("tab_f", [P, 2, NST], F32)
        tab = place("tab", [P, 2, NST], I32)
        slot_w = place("slot_w", [P, NTAB], F32)
        id_f = [place(f"id_f{n}", [P, NTAB], F32) for n in range(3)]
        ids = place("ids", [P, NTAB], U32)
        gather_ids = place("gather_ids", [P, TPS], U32)
        scatter_ids = place("scatter_ids", [P, TPS], U32)
        assert at[0] <= nc.sbuf_usable_end, (at[0], nc.sbuf_usable_end)

        def psum(name):
            return ctx.enter_context(nc.psum_tensor(name, [P, D], F32))

        ab = [psum(f"ab{b}") for b in range(2)]
        gT_ps = psum("gT_ps")
        out_ps = [psum(f"out_ps{j}") for j in range(TPS)]
        decay_ps = [gT_ps, out_ps[TPS - 1]]
        logits = out_ps[0][:, 0:NT * E]
        prefix_ps = out_ps[1][:, 0:NT * E]
        total_ps = out_ps[2][:, 0:NT * E]
        table_ps = out_ps[3][:, 0:2 * NTAB]

        def sem(name):
            return ctx.enter_context(nc.semaphore(name))

        x_loaded = [sem(f"x_loaded{n}") for n in range(NG)]
        small_loaded = sem("small_loaded")
        consts_ready = sem("consts_ready")
        dve_step = sem("dve_step")
        decay_ready = sem("decay_ready")
        ve_ready = sem("ve_ready")
        sd_ready = sem("sd_ready")
        xn_ready = sem("xn_ready")
        xn_stored = [sem(f"xn_stored{q}") for q in range(G)]
        xnT_full = sem("xnT_full")
        xnT_ready = sem("xnT_ready")
        logits_full = sem("logits_full")
        decay_full = sem("decay_full")
        decay_added = sem("decay_added")
        base_ready = sem("base_ready")
        base_stored = sem("base_stored")
        spare_stored = sem("spare_stored")
        shifted_ready = sem("shifted_ready")
        exp_ready = sem("exp_ready")
        chosen_ready = sem("chosen_ready")
        prefix_full = sem("prefix_full")
        tab_ready = sem("tab_ready")
        pick_ready = sem("pick_ready")
        table_full = sem("table_full")
        ids_ready = sem("ids_ready")
        raw_loaded = [sem(f"raw_loaded{b}") for b in range(3)]
        hi13_done = sem("hi13_done")
        hi2_done = sem("hi2_done")
        lo13_done = sem("lo13_done")
        lo2_done = sem("lo2_done")
        chunk_used = sem("chunk_used")
        ids_copied = sem("ids_copied")
        gathered = [sem(f"gathered{j}") for j in range(TPS)]
        xT_full = sem("xT_full")
        xT_hi_done = sem("xT_hi_done")
        xT_ready = sem("xT_ready")
        ab_full = sem("ab_full")
        silu_ready = sem("silu_ready")
        g_ready = sem("g_ready")
        gT_full = sem("gT_full")
        gT_hi_done = sem("gT_hi_done")
        gT_ready = sem("gT_ready")
        out_full = sem("out_full")
        y_ready = sem("y_ready")
        y_added = sem("y_added")

        NT_ROW, EXPERT_ROW = 0, 1

        def tiles_of(eng, s):
            return eng.value_load(tab[0:1, NT_ROW, ds(s, 1)], min_val=0, max_val=TPS)

        def expert_of(eng, s):
            return eng.value_load(tab[0:1, EXPERT_ROW, ds(s, 1)], min_val=0, max_val=E - 1)

        def for_tiles(eng, nt, body, between=None):
            for j in reversed(range(TPS)):
                if j:
                    with eng.If(nt > j):
                        body(j)
                else:
                    body(j)
                if between:
                    between(TPS - 1 - j)

        def bc(ap, shape):
            return ap.to_broadcast(shape)

        block = ctx.enter_context(nc.Block())

        @block.sync
        def _(sp):
            for n in range(NG):
                sp.dma_start(xs[:, n * G:(n + 1) * G, :], x_tiles[n]).then_inc(x_loaded[n], 16)
            with sp.Fori(0, NG) as i:
                for q in range(G):
                    sp.wait_ge(xn_ready, i * G + q + 1)
                    sp.dma_start(xn_tiles[ds(i * G + q, 1)].rearrange("a p d -> (a p) d"),
                                 xn[q][:, :]).then_inc(xn_stored[q], 16)
            with sp.Fori(0, NG) as i:
                sp.wait_ge(base_ready, (i + 1) * G)
                sp.dma_start(out_tiles[ds(i, 1)].rearrange("a p q d -> (a p) q d"),
                             xs[:, ds(i * G, G), :]).then_inc(base_stored, 16)
            sp.wait_ge(tab_ready, 1)

            def load_chunk(expert, c, buf):
                w13_dst = raw[buf][:, 0:W13].rearrange("p (k h m) -> p k h m", k=DC, h=2)
                for h, w in enumerate((w1, w3)):
                    src = w[ds(expert, 1), :, c * MC:(c + 1) * MC].rearrange("a (k p) m -> (a p) k m", p=P)
                    sp.dma_start(w13_dst[:, :, h, :], src).then_inc(raw_loaded[buf], 16)
                src = w2[ds(expert, 1), c * MC:(c + 1) * MC, :].rearrange("a (k p) d -> (a p) k d", p=P)
                sp.dma_start(raw[buf][:, W13:W13 + W2E].rearrange("p (k d) -> p k d", k=MP), src)\
                    .then_inc(raw_loaded[buf], 16)

            expert = expert_of(sp, 0)
            for n in range(2):
                load_chunk(expert, n, RAW_BUF[n])
            with sp.Fori(0, NS) as s:
                with sp.If(tiles_of(sp, s) > 0):
                    expert = expert_of(sp, s)
                    for n in range(2, NCH + 2):
                        c = n % NCH
                        sp.wait_ge(lo13_done, s * NCH + (n + 1 - RAW_DIST[c] + RAW_CREDIT))
                        sp.wait_ge(lo2_done, s * NCH + (n + 1 - RAW_DIST[c] + RAW_CREDIT))
                        if n == NCH:
                            expert = expert_of(sp, s + 1)
                        load_chunk(expert, c, RAW_BUF[c])

        @block.gpsimd
        def _(pool):
            pool.memset(zeros[:, :], 0.0).then_inc(consts_ready, 1)
            pool.memset(ones_row[:, :], 1.0).then_inc(consts_ready, 1)
            pool.memset(ones[:, :], 1.0).then_inc(consts_ready, 1)
            pool.iota(lane_iota[:, :], pattern=[[1, P]], base=0, channel_multiplier=0,
                      allow_small_or_imprecise_dtypes=True).then_inc(consts_ready, 1)
            pool.iota(token1[:, :], pattern=[[P, NT]], base=1, channel_multiplier=1,
                      allow_small_or_imprecise_dtypes=True).then_inc(consts_ready, 1)
            pool.iota(rev[:, :], pattern=[[-1, E]], base=E, channel_multiplier=0,
                      allow_small_or_imprecise_dtypes=True).then_inc(consts_ready, 1)
            pool.iota(sb_iota[:, :], pattern=[[1, NST]], base=0, channel_multiplier=0,
                      allow_small_or_imprecise_dtypes=True).then_inc(consts_ready, 1)
            pool.iota(spare[:, :], pattern=[[0, 1]], base=T, channel_multiplier=1,
                      allow_small_or_imprecise_dtypes=True).then_inc(consts_ready, 1)
            pool.wait_ge(consts_ready, 8)
            pool.affine_select(out=diagonal[:, :], in_=ones_row[:, :], compare_op=ALU.is_equal, fill=0.0, base=0,
                               pattern=[[-1, D]], channel_multiplier=1).then_inc(consts_ready, 1)
            pool.affine_select(out=ident[:, :], in_=ones[:, :], compare_op=ALU.is_equal, fill=0.0, base=0,
                               pattern=[[-1, P]], channel_multiplier=1).then_inc(consts_ready, 1)
            pool.affine_select(out=before[:, :], in_=ones[:, :], compare_op=ALU.is_gt, fill=0.0, base=0,
                               pattern=[[1, P]], channel_multiplier=-1).then_inc(consts_ready, 1)
            pool.memset(scrap[:, 0:1], 0.0).then_inc(chunk_used, USED_CREDIT)
            pool.memset(scrap[:, 1:2], 0.0).then_inc(lo2_done, RAW_CREDIT)
            pool.memset(scrap[:, 2:4], 0.0).then_inc(y_ready, Y_CREDIT)
            pool.dma_start(xn_dram[T:T + P, :], zeros[:, :]).then_inc(spare_stored, 16)
            pool.dma_start(out[T:T + P, :], zeros[:, :]).then_inc(spare_stored, 16)
            pool.wait_ge(small_loaded, 5 * 16)
            with pool.Fori(0, NG) as i:
                for q in range(G):
                    pool.wait_ge(decay_added, i * G + (q + 1 + DECAY_CREDIT))
                    xt = xs[:, ds(i * G + q, 1), :].rearrange("p a d -> p (a d)")
                    pool.tensor_tensor(xt, xt, bias_row[:, :], ALU.add).then_inc(base_ready, 1)

            def lo2(c, s, n):
                pool.wait_ge(hi2_done, s * NCH + (n + 1))
                pool.tensor_tensor(w2_lo[W2_BUF[c]][:, :], raw[RAW_BUF[c]][:, W13:W13 + W2E],
                                   w2_hi[W2_BUF[c]][:, :].bitcast(F32), ALU.subtract).then_inc(lo2_done, 1)

            def gather(s):
                pool.tensor_copy(gather_ids[:, :], ids[:, ds(s * TPS, TPS)]).then_inc(ids_copied, 1)
                pool.reg_add(copies, copies, 1)
                for j in reversed(range(TPS)):
                    pool.wait_ge(spare_stored, 32)
                    pool.wait_ge(ids_copied, copies)
                    pool.indirect_dma_start(xg[j][:, :], None, xn_dram,
                                            bass.IndirectOffsetOnAxis(ap=gather_ids[:, j:j + 1], axis=0))\
                        .then_inc(gathered[j], 16)

            added = pool.alloc_register("added")
            computed = pool.alloc_register("computed")
            copies = pool.alloc_register("copies")
            for r, start in ((added, 0), (computed, Y_CREDIT), (copies, 0)):
                pool.reg_mov(r, start)
            pool.wait_ge(ids_ready, 1)
            for q in range(G):
                pool.wait_ge(xn_stored[q], 16 * NG + XN_CREDIT)
            pool.wait_ge(spare_stored, 32)
            pool.wait_ge(base_stored, 16 * NG)
            gather(0)
            lo2(0, 0, 0)
            with pool.Fori(0, NS) as s:
                nt = tiles_of(pool, s)
                with pool.If(nt > 0):
                    for n in range(1, NCH + 1):
                        lo2(n % NCH, s, n)
                        if n == 2:
                            pool.wait_ge(xT_full, s * TPS + TPS)
                            gather(s + 1)
                        if n == 1:
                            with pool.If(s > 0):
                                pool.wait_ge(y_added, added)
                            pool.tensor_copy(scatter_ids[:, :], ids[:, ds(s * TPS, TPS)]).then_inc(ids_copied, 1)
                            pool.reg_add(copies, copies, 1)
                            pool.wait_ge(ids_copied, copies)

                    def add(j):
                        pool.reg_add(computed, computed, 1)
                        pool.reg_add(added, added, 16)
                        pool.wait_ge(spare_stored, 32)
                        pool.wait_ge(y_ready, computed)
                        pool.indirect_dma_start(out, bass.IndirectOffsetOnAxis(ap=scatter_ids[:, j:j + 1], axis=0),
                                                y[j][:, :], None, compute_op=ALU.add).then_inc(y_added, 16)

                    for_tiles(pool, nt, add)
            pool.wait_ge(y_added, added)

        @block.scalar
        def _(act):
            act.dma_start(dv[:, :], decay_value.rearrange("k a -> a k").to_broadcast([P, 2])).then_inc(small_loaded, 16)
            act.dma_start(w1_row[:, :], weight[1:2, :].to_broadcast([P, D])).then_inc(small_loaded, 16)
            act.dma_start(bias_row[:, :], bias.rearrange("(a d) -> a d", a=1).to_broadcast([P, D]))\
                .then_inc(small_loaded, 16)
            act.dma_start(w0_col[:, :], weight[0, :].rearrange("(k p) -> p k", p=P)).then_inc(small_loaded, 16)
            act.dma_start(gate[:, :, :], gate_w.rearrange("(k p) e -> p k e", p=P)).then_inc(small_loaded, 16)
            act.wait_ge(ve_ready, 1)
            act.activation(sd[:, :], ve[:, :], ACT.Sqrt).then_inc(sd_ready, 1)
            with act.Fori(0, NG) as i:
                for q in range(G):
                    act.wait_ge(xnT_full, i * G + q + 1)
                    act.activation(xnT[q][:, :, :].rearrange("p k t -> p (k t)"), ab[q % 2][:, :], ACT.Copy)\
                        .then_inc(xnT_ready, 1)
            act.wait_ge(shifted_ready, 1)
            act.activation(R[1][:, :, :], R[0][:, :, :], ACT.Exp).then_inc(exp_ready, 1)

            def hi13(s, n, h):
                c = n % NCH
                b = RAW_BUF[c]
                loads = sum(RAW_BUF[m % NCH] == b for m in range(n + 1))
                act.wait_ge(raw_loaded[b], s * (48 * RAW_BUF.count(b)) + 48 * loads)
                part = slice(h * W13 // 2, (h + 1) * W13 // 2)
                act.activation(w13_hi[W13_BUF[c]][:, part], raw[b][:, part], ACT.Copy).then_inc(hi13_done, 1)

            def hi2(s, n):
                c = n % NCH
                if n:
                    act.wait_ge(chunk_used, s * (NCH - 1) + (w2_used(n - W2_DIST[c]) + USED_CREDIT))
                act.activation(w2_hi[W2_BUF[c]][:, :], raw[RAW_BUF[c]][:, W13:W13 + W2E], ACT.Copy)\
                    .then_inc(hi2_done, 1)

            def turn_hi(s, n):
                j = TPS - 1 - n
                act.wait_ge(xT_full, s * TPS + (n + 1))
                act.activation(xT_hi[j][:, :, :].rearrange("p k t -> p (k t)"), ab[j % 2][:, :], ACT.Copy)\
                    .then_inc(xT_hi_done, 1)

            act.wait_ge(tab_ready, 1)
            act.wait_ge(y_ready, Y_CREDIT)
            act.activation(scrap[:, 4:5], scrap[:, 3:4], ACT.Silu)
            for n in range(2):
                for h in range(2):
                    hi13(0, n, h)
                if n == 0:
                    hi2(0, 0)
            act.wait_ge(base_stored, 16 * NG)
            for n in range(TPS):
                turn_hi(0, n)
            units = act.alloc_register("act_units")
            turned = act.alloc_register("act_turned")
            tiles = act.alloc_register("act_tiles")
            for r in (units, turned, tiles):
                act.reg_mov(r, 0)
            with act.Fori(0, NS) as s:
                nt = tiles_of(act, s)
                with act.If(nt > 0):
                    for step in range(NCH + 1):
                        def unit(j):
                            if step > 0:
                                act.reg_add(turned, turned, 1)
                                act.wait_ge(gT_full, turned)
                                act.activation(gT_hi[j][:, :, :].rearrange("p k t -> p (k t)"),
                                               gT_ps[:, 0:MC], ACT.Copy).then_inc(gT_hi_done, 1)
                            if step < NCH:
                                act.reg_add(units, units, 1)
                                act.wait_ge(ab_full, units)
                                act.activation(silu[j % 2][:, :], ab[j % 2][:, 0:MC], ACT.Silu)\
                                    .then_inc(silu_ready, 1)

                        def split(place):
                            if step == NCH:
                                turn_hi(s + 1, place)
                            elif place in (1, 2):
                                hi13(s, step + 2, place - 1)
                            elif place == 3:
                                hi2(s, step + 1)

                        for_tiles(act, nt, unit, split)

                    def result(j):
                        act.reg_add(tiles, tiles, 1)
                        act.wait_ge(out_full, tiles)
                        act.wait_ge(ids_copied, s * 2 + 2)
                        act.activation(y[j][:, :], out_ps[j][:, :], ACT.Copy,
                                       scale=slot_w[:, ds(s * TPS + j, 1)]).then_inc(y_ready, 1)

                    for_tiles(act, nt, result)

        @block.vector
        def _(dve):
            steps = [0]

            def chain(ins):
                steps[0] += 1
                ins.then_inc(dve_step, 1)
                dve.wait_ge(dve_step, steps[0])

            dve.memset(scrap[:, 8:9], 0.0).then_inc(decay_added, DECAY_CREDIT)
            dve.memset(scrap[:, 9:10], 0.0).then_inc(lo13_done, RAW_CREDIT)
            dve.memset(scrap[:, 10:11], 0.0).then_inc(g_ready, G_CREDIT)
            dve.memset(scrap[:, 11:12], 0.0).then_inc(gT_ready, GT_CREDIT)
            for q in range(G):
                dve.memset(scrap[:, 12 + q:13 + q], 0.0).then_inc(xn_stored[q], XN_CREDIT)
            dve.wait_ge(small_loaded, 5 * 16)
            chain(dve.tensor_scalar(dv[:, :], dv[:, :], 0.9, 1.0, ALU.max, ALU.min))
            dve.wait_ge(consts_ready, 11)
            for k in range(2):
                last = dve.tensor_tensor_scan(power[k][:, :], bc(dv[:, k:k + 1], [P, D]), diagonal[:, :], 0.0,
                                              ALU.mult, ALU.add)
            chain(last)
            for k in range(DC):
                n = D - k * P
                last = dve.tensor_tensor(decay[:, k, 0:n], power[1][:, 0:n], w1_row[:, k * P:D], ALU.mult)
            chain(last)
            for k in range(DC):
                n = D - k * P
                dve.scalar_tensor_tensor(decay[:, k, 0:n], power[0][:, 0:n], w0_col[:, k:k + 1],
                                         decay[:, k, 0:n], ALU.mult, ALU.add).then_inc(decay_ready, 1)
            for n in range(NG):
                dve.wait_ge(x_loaded[n], 16)
                for t in range(n * G, (n + 1) * G):
                    last = dve.bn_stats(stats[:, t, :], xs[:, t, :])
            chain(last)
            for t in range(NT):
                last = dve.bn_aggr(mv[:, t, :], stats[:, t, :])
            chain(last)
            dve.tensor_scalar(ve[:, :], mv[:, :, 1], EPS, None, ALU.add).then_inc(ve_ready, 1)
            dve.wait_ge(ve_ready, 1)
            dve.wait_ge(sd_ready, 1)
            chain(dve.reciprocal(rs[:, :], sd[:, :]))
            chain(dve.tensor_tensor(nt1[:, :], rs[:, :], rs[:, :], ALU.mult))
            chain(dve.tensor_tensor(nt1[:, :], nt1[:, :], ve[:, :], ALU.mult))
            chain(dve.tensor_scalar(nt1[:, :], nt1[:, :], -0.5, 1.5, ALU.mult, ALU.add))
            chain(dve.tensor_tensor(rstd[:, :], rs[:, :], nt1[:, :], ALU.mult))

            def normalize(i, q):
                dve.wait_ge(xn_stored[q], i * 16 + XN_CREDIT)
                t = i * G + q
                dve.tensor_scalar(xn[q][:, :], xs[:, ds(t, 1), :].rearrange("p a d -> p (a d)"),
                                  mv[:, ds(t, 1), 0], rstd[:, ds(t, 1)],
                                  ALU.subtract, ALU.mult).then_inc(xn_ready, 1)

            dve.tensor_scalar(xn[0][:, :], xs[:, 0, :], mv[:, 0, 0:1], rstd[:, 0:1],
                              ALU.subtract, ALU.mult).then_inc(xn_ready, 1)
            with dve.Fori(0, NG) as i:
                for q in range(G):
                    if q < G - 1:
                        normalize(i, q + 1)
                    else:
                        with dve.If(i < NG - 1):
                            normalize(nc.s_assert_within(i + 1, 1, NG - 1), 0)
                    dve.wait_ge(decay_full, i * G + q + 1)
                    xt = xs[:, ds(i * G + q, 1), :].rearrange("p a d -> p (a d)")
                    dve.tensor_tensor(xt, decay_ps[q % 2][:, :], xt, ALU.add).then_inc(decay_added, 1)

            te = [P, NT, E]

            def over_e(v):
                return bc(v[:, :].unsqueeze(2), te)

            def by_e(v):
                return bc(v[:, :].unsqueeze(1), te)

            dve.wait_ge(logits_full, NT)
            lg = logits.rearrange("p (t e) -> p t e", e=E)
            chain(dve.tensor_reduce(V[0][:, :], lg, AX_X, ALU.max))
            dve.tensor_tensor(R[0][:, :, :], lg, over_e(V[0]), ALU.subtract).then_inc(shifted_ready, 1)
            dve.wait_ge(exp_ready, 1)
            chain(dve.tensor_reduce(V[1][:, :], R[1][:, :, :], AX_X, ALU.add))
            chain(dve.reciprocal(V[2][:, :], V[1][:, :]))
            chain(dve.tensor_tensor(R[2][:, :, :], R[1][:, :, :], over_e(V[2]), ALU.mult))
            for k, (p, hot) in enumerate(((2, 4), (5, 6))):
                chain(dve.tensor_reduce(V[3 + k][:, :], R[p][:, :, :], AX_X, ALU.max))
                chain(dve.tensor_tensor(R[3][:, :, :], R[p][:, :, :], over_e(V[3 + k]), ALU.is_equal))
                chain(dve.tensor_tensor(R[3][:, :, :], R[3][:, :, :], by_e(rev), ALU.mult))
                chain(dve.tensor_reduce(V[5][:, :], R[3][:, :, :], AX_X, ALU.max))
                chain(dve.tensor_tensor(R[hot][:, :, :], by_e(rev), over_e(V[5]), ALU.is_equal))
                if k == 0:
                    chain(dve.scalar_tensor_tensor(R[5][:, :, :], R[4][:, :, :], -2.0, R[2][:, :, :],
                                                   ALU.mult, ALU.add))
            dve.tensor_tensor(R[7][:, :, :], R[4][:, :, :], R[6][:, :, :], ALU.add).then_inc(chosen_ready, 1)
            chain(dve.tensor_tensor(V[5][:, :], V[3][:, :], V[4][:, :], ALU.add))
            chain(dve.reciprocal(V[6][:, :], V[5][:, :]))
            dve.tensor_tensor(top_w[:, 0, :], V[3][:, :], V[6][:, :], ALU.mult)
            chain(dve.tensor_tensor(top_w[:, 1, :], V[4][:, :], V[6][:, :], ALU.mult))

            dve.wait_ge(prefix_full, 1)
            chain(dve.tensor_copy(R[0][:, :, :], total_ps.rearrange("p (t e) -> p t e", e=E)))
            a, b, k = 0, 1, 1
            while k < NT:
                dve.tensor_copy(R[b][:, 0:k, :], R[a][:, 0:k, :])
                chain(dve.tensor_tensor(R[b][:, k:NT, :], R[a][:, k:NT, :], R[a][:, 0:NT - k, :], ALU.add))
                a, b, k = b, a, 2 * k
            upto, rank = R[a], R[b]
            count = C[0]
            chain(dve.tensor_copy(count[:, :], upto[:, NT - 1, :]))
            chain(dve.tensor_tensor(rank[:, :, :], upto[:, :, :], total_ps.rearrange("p (t e) -> p t e", e=E),
                                    ALU.subtract))
            chain(dve.tensor_tensor(rank[:, :, :], rank[:, :, :], prefix_ps.rearrange("p (t e) -> p t e", e=E),
                                    ALU.add))
            chain(dve.tensor_scalar(C[1][:, :], count[:, :], 0.0, None, ALU.is_gt))
            n_sb, other = C[1], C[2]
            for k in range(1, MAX_SB):
                chain(dve.scalar_tensor_tensor(other[:, :], count[:, :], float(k * SLOTS), n_sb[:, :],
                                               ALU.is_gt, ALU.add))
                n_sb, other = other, n_sb
            a, b, k = n_sb, C[3], 1
            spare_c = [C[4], C[5]]
            while k < E:
                dve.tensor_copy(b[:, 0:k], a[:, 0:k])
                chain(dve.tensor_tensor(b[:, k:E], a[:, k:E], a[:, 0:E - k], ALU.add))
                a, b, k = b, spare_c.pop() if spare_c else None, 2 * k
            sb_end = a
            first_sb = C[6]
            chain(dve.tensor_tensor(first_sb[:, :], sb_end[:, :], n_sb[:, :], ALU.subtract))
            first_slot = C[7]
            chain(dve.tensor_scalar(first_slot[:, :], first_sb[:, :], float(SLOTS), None, ALU.mult))

            se = [P, NST, E]
            s_row = bc(sb_iota[:, :].unsqueeze(2), se)
            chain(dve.tensor_tensor(Q[0][:, :, :], s_row, bc(sb_end[:, :].unsqueeze(1), se), ALU.is_ge))
            chain(dve.tensor_reduce(tab_f[:, EXPERT_ROW, :], Q[0][:, :, :], AX_X, ALU.add))
            dve.tensor_scalar(tab_f[:, EXPERT_ROW, :], tab_f[:, EXPERT_ROW, :], float(E - 1), None, ALU.min)
            chain(dve.tensor_tensor(Q[0][:, :, :], s_row, bc(first_sb[:, :].unsqueeze(1), se), ALU.subtract))
            chain(dve.scalar_tensor_tensor(Q[1][:, :, :], Q[0][:, :, :], -float(SLOTS),
                                           bc(count[:, :].unsqueeze(1), se), ALU.mult, ALU.add))
            chain(dve.tensor_scalar(Q[2][:, :, :], Q[1][:, :, :], 0.0, None, ALU.is_gt))
            for k in range(1, TPS):
                chain(dve.scalar_tensor_tensor(Q[2][:, :, :], Q[1][:, :, :], float(k * P), Q[2][:, :, :],
                                               ALU.is_gt, ALU.add))
            chain(dve.scalar_tensor_tensor(Q[1][:, :, :], Q[0][:, :, :], 0.0, Q[2][:, :, :],
                                           ALU.is_ge, ALU.mult))
            chain(dve.tensor_reduce(tab_f[:, NT_ROW, :], Q[1][:, :, :], AX_X, ALU.add))
            dve.tensor_copy(tab[:, :, :], tab_f[:, :, :]).then_inc(tab_ready, 1)

            chain(dve.tensor_tensor(rank[:, :, :], rank[:, :, :], by_e(first_slot), ALU.add))
            for k, hot in enumerate((4, 6)):
                chain(dve.tensor_tensor(R[3 + 2 * k][:, :, :], R[hot][:, :, :], rank[:, :, :], ALU.mult))
                chain(dve.tensor_reduce(slot_f[:, k, :], R[3 + 2 * k][:, :, :], AX_X, ALU.add))
            chain(dve.tensor_copy(slot_i[:, :, :], slot_f[:, :, :]))
            lanes = P - 1
            dve.tensor_scalar(lane_i[:, :, :], slot_i[:, :, :], lanes, None, ALU.bitwise_and)
            chain(dve.tensor_scalar(tile_i[:, :, :], slot_i[:, :, :], lanes.bit_length(), None,
                                    ALU.logical_shift_right))
            dve.tensor_copy(lane_f[:, :, :], lane_i[:, :, :])
            chain(dve.tensor_copy(tile_f[:, :, :], tile_i[:, :, :]))
            for q in range(G):
                dve.wait_ge(xn_stored[q], 16 * NG + XN_CREDIT)
            for k in range(TOP_K):
                for t in range(NT):
                    kt = k * NT + t
                    dve.tensor_scalar(pick_lane[:, kt, :], lane_iota[:, :], lane_f[:, k, t:t + 1], None,
                                      ALU.is_equal)
                    dve.tensor_scalar(pick_tile[:, kt, 0, :], lane_iota[:, 0:NTAB], tile_f[:, k, t:t + 1],
                                      token1[:, t:t + 1], ALU.is_equal, ALU.mult)
                    dve.tensor_scalar(pick_tile[:, kt, 1, :], lane_iota[:, 0:NTAB], tile_f[:, k, t:t + 1],
                                      top_w[:, k, t:t + 1], ALU.is_equal, ALU.mult).then_inc(pick_ready, 1)

            def lo13(c, s, n, h):
                part = slice(h * W13 // 2, (h + 1) * W13 // 2)
                dve.wait_ge(hi13_done, s * (2 * NCH) + (2 * n + h + 1))
                ins = dve.tensor_tensor(w13_lo[W13_BUF[c]][:, part], raw[RAW_BUF[c]][:, part],
                                        w13_hi[W13_BUF[c]][:, part].bitcast(F32), ALU.subtract)
                if h == 1:
                    ins.then_inc(lo13_done, 1)

            for n in range(2):
                for h in range(2):
                    lo13(n, 0, n, h)
            dve.wait_ge(table_full, 1)
            id1 = table_ps[:, 0:NTAB]
            dve.tensor_copy(slot_w[:, :], table_ps[:, NTAB:2 * NTAB])
            dve.tensor_scalar(id_f[0][:, :], id1, 0.0, spare[:, 0:1], ALU.is_equal, ALU.mult)
            chain(dve.tensor_scalar(id_f[1][:, :], id1, -1.0, 0.0, ALU.add, ALU.max))
            chain(dve.tensor_tensor(id_f[2][:, :], id_f[0][:, :], id_f[1][:, :], ALU.add))
            dve.tensor_copy(ids[:, :], id_f[2][:, :]).then_inc(ids_ready, 1)

            def turn_lo(s, n):
                j = TPS - 1 - n
                dve.wait_ge(xT_hi_done, s * TPS + (n + 1))
                dve.tensor_tensor(xT_lo[j][:, :, :].rearrange("p k t -> p (k t)"), ab[j % 2][:, :],
                                  xT_hi[j][:, :, :].rearrange("p k t -> p (k t)").bitcast(F32),
                                  ALU.subtract).then_inc(xT_ready, 1)

            for n in range(TPS):
                turn_lo(0, n)
            units = dve.alloc_register("dve_units")
            turned = dve.alloc_register("dve_turned")
            dve.reg_mov(units, 0)
            dve.reg_mov(turned, 0)
            with dve.Fori(0, NS) as s:
                nt = tiles_of(dve, s)
                with dve.If(nt > 0):
                    for step in range(NCH + 1):
                        def unit(j):
                            if step > 0:
                                dve.reg_add(turned, turned, 1)
                                dve.wait_ge(gT_hi_done, turned)
                                dve.tensor_tensor(gT_lo[j][:, :, :].rearrange("p k t -> p (k t)"),
                                                  gT_ps[:, 0:MC],
                                                  gT_hi[j][:, :, :].rearrange("p k t -> p (k t)").bitcast(F32),
                                                  ALU.subtract).then_inc(gT_ready, 1)
                            if step < NCH:
                                dve.reg_add(units, units, 1)
                                dve.wait_ge(silu_ready, units)
                                dve.tensor_tensor(g[j][:, :], ab[j % 2][:, MC:2 * MC], silu[j % 2][:, :],
                                                  ALU.mult).then_inc(g_ready, 1)

                        def split(place):
                            n = step + 2
                            if step == NCH:
                                turn_lo(s + 1, place)
                            elif place in (1, 2):
                                lo13(n % NCH, s, n, place - 1)

                        for_tiles(dve, nt, unit, split)

        @block.tensor
        def _(pe):
            def turn(dst, src, *done):
                for k in range(DC):
                    last = pe.transpose(dst[:, k * P:(k + 1) * P], src[:, k * P:(k + 1) * P], ident[:, :])
                last.then_inc(*done)

            def turn_xn(i, q):
                pe.wait_ge(xn_ready, i * G + q + 1)
                turn(ab[q % 2], xn[q], xnT_full, 1)

            pe.wait_ge(consts_ready, 11)
            pe.wait_ge(small_loaded, 5 * 16)
            pe.wait_ge(xn_ready, 1)
            turn(ab[0], xn[0], xnT_full, 1)
            pe.wait_ge(decay_ready, DC)
            with pe.Fori(0, NG) as i:
                for q in range(G):
                    if q < G - 1:
                        turn_xn(i, q + 1)
                    else:
                        with pe.If(i < NG - 1):
                            turn_xn(i + 1, 0)
                    pe.wait_ge(xnT_ready, i * G + q + 1)
                    for k in range(DC):
                        last = pe.matmul(logits[:, ds((i * G + q) * E, E)], xnT[q][:, k, :], gate[:, k, :],
                                         start=(k == 0), stop=(k == DC - 1))
                    last.then_inc(logits_full, 1)
                    pe.wait_ge(decay_added, i * G + (q - 1 + DECAY_CREDIT))
                    for k in range(DC):
                        last = pe.matmul(decay_ps[q % 2][:, k * P:D], xnT[q][:, k, :], decay[:, k, 0:D - k * P],
                                         start=(k == 0), stop=(k == DC - 1), skip_group_check=True)
                    last.then_inc(decay_full, 1)
            pe.wait_ge(chosen_ready, 1)
            chosen = R[7][:, :, :].rearrange("p t e -> p (t e)")
            pe.matmul(prefix_ps, before[:, :], chosen, start=True, stop=True)
            pe.matmul(total_ps, ones[:, :], chosen, start=True, stop=True).then_inc(prefix_full, 1)
            for kt in range(NKT):
                pe.wait_ge(pick_ready, kt + 1)
                last = pe.matmul(table_ps, pick_lane[:, kt, :],
                                 pick_tile[:, kt, :, :].rearrange("p a n -> p (a n)"),
                                 start=(kt == 0), stop=(kt == NKT - 1))
            last.then_inc(table_full, 1)

            def turn_rows(s, n):
                j = TPS - 1 - n
                pe.wait_ge(gathered[j], s * 16 + 16)
                if n >= 2:
                    pe.wait_ge(xT_ready, s * TPS + (n - 1))
                turn(ab[j % 2], xg[j], xT_full, 1)

            for n in range(TPS):
                turn_rows(0, n)
            before_last = pe.alloc_register("before_last")
            all_g = pe.alloc_register("all_g")
            all_gT = pe.alloc_register("all_gT")
            this_gT = pe.alloc_register("this_gT")
            tiles = pe.alloc_register("tiles")
            for r, start in ((before_last, G_CREDIT - 1), (all_g, G_CREDIT), (all_gT, GT_CREDIT),
                             (this_gT, GT_CREDIT + 1), (tiles, Y_CREDIT)):
                pe.reg_mov(r, start)

            def turn_g(j):
                pe.wait_ge(gT_ready, all_gT)
                for k in range(MP):
                    last = pe.transpose(gT_ps[:, k * P:(k + 1) * P], g[j][:, k * P:(k + 1) * P], ident[:, :])
                last.then_inc(gT_full, 1)
                pe.reg_add(all_gT, all_gT, 1)

            def up(c, j):
                w_hi, w_lo = w13_hi[W13_BUF[c]], w13_lo[W13_BUF[c]]
                pe.wait_ge(g_ready, before_last)
                n = 0
                for k in range(DC):
                    part = slice(k * 2 * MC, (k + 1) * 2 * MC)
                    for lhs, rhs in ((xT_hi, w_hi), (xT_hi, w_lo), (xT_lo, w_hi)):
                        last = pe.matmul(ab[j % 2][:, :], lhs[j][:, k, :], rhs[:, part],
                                         start=(n == 0), stop=(n == 3 * DC - 1))
                        n += 1
                last.then_inc(ab_full, 1)
                pe.reg_add(before_last, before_last, 1)
                pe.reg_add(all_g, all_g, 1)

            def down(c, j):
                v_hi, v_lo = w2_hi[W2_BUF[c]], w2_lo[W2_BUF[c]]
                pe.wait_ge(gT_ready, this_gT)
                pe.reg_add(this_gT, this_gT, 1)
                n = 0
                for k in range(MP):
                    part = slice(k * D, (k + 1) * D)
                    for lhs, rhs in ((gT_hi, v_hi), (gT_hi, v_lo), (gT_lo, v_hi)):
                        last = pe.matmul(out_ps[j][:, :], lhs[j][:, k, :], rhs[:, part],
                                         start=(c == 0 and n == 0),
                                         stop=(c == NCH - 1 and n == 3 * MP - 1))
                        n += 1
                if c == NCH - 1:
                    last.then_inc(out_full, 1)
                    pe.reg_add(tiles, tiles, 1)
                elif j == 0:
                    last.then_inc(chunk_used, 1)

            with pe.Fori(0, NS) as s:
                nt = tiles_of(pe, s)
                with pe.If(nt > 0):
                    for step in range(NCH):
                        pe.wait_ge(g_ready, all_g)
                        pe.wait_ge(lo13_done, s * NCH + (step + 1 + RAW_CREDIT))
                        if step == 0:
                            pe.wait_ge(xT_ready, s * TPS + TPS)

                        def unit(j):
                            if step > 0:
                                turn_g(j)
                            up(step, j)

                        for_tiles(pe, nt, unit)
                        if step > 0:
                            pe.wait_ge(lo2_done, s * NCH + (step + RAW_CREDIT))
                            if step == 1:
                                pe.wait_ge(y_ready, tiles)
                            for_tiles(pe, nt, lambda j: down(step - 1, j))
                    pe.wait_ge(g_ready, all_g)
                    pe.wait_ge(lo2_done, s * NCH + (NCH + RAW_CREDIT))

                    def finish(place):
                        turn_rows(s + 1, place)
                        if place:
                            tile = TPS - place
                            with pe.If(nt > tile):
                                down(NCH - 1, tile)

                    for_tiles(pe, nt, turn_g, finish)
                    down(NCH - 1, 0)


_INS = ['L0_attn_x', 'L0_attn_weight', 'L0_attn_bias', 'L0_attn_decay_value', 'L0_ffn_gate_w',
        'L0_ffn_w1', 'L0_ffn_w2', 'L0_ffn_w3']


def kernel(**inputs):
    import numpy as _np
    import concourse.bacc as _bacc
    from concourse import mybir as _mybir
    from concourse.bass_utils import run_bass_kernel_spmd as _run

    nc = _bacc.Bacc("TRN2", target_bir_lowering=False, num_devices=1)
    arrays, args = {}, []
    for name in _INS:
        a = _np.ascontiguousarray(inputs[name])
        arrays[f"in_{name}_dram"] = a
        args.append(nc.dram_tensor(f"in_{name}_dram", a.shape, _mybir.dt.from_np(a.dtype), kind="ExternalInput").ap())
    B, S, D = inputs['L0_attn_x'].shape
    out = nc.dram_tensor("out_0_dram", (B * S + 128, D), _mybir.dt.from_np(_np.dtype('float32')),
                         kind="ExternalOutput").ap()
    decay_moe_kernel(nc, *args, out)
    r = _run(nc, [arrays], core_ids=[0])
    return r.results[0]["out_0_dram"][:B * S].reshape(B, S, D)
```

```python
from contextlib import ExitStack

import concourse.bass as bass
from concourse import mybir

F32 = mybir.dt.float32
F32R = mybir.dt.float32r
I32 = mybir.dt.int32
U32 = mybir.dt.uint32
ALU = mybir.AluOpType
ACT = mybir.ActivationFunctionType
AX_X = mybir.AxisListType.X
ds = bass.ds

P = 128
TOP_K = 2
EPS = 1e-5
TPS = 5

RAW_BUF = [0, 1, 2, 0, 1, 2, 1]
W13_BUF = [0, 1, 2, 0, 1, 2, 3]
W2_BUF = [0, 1, 2, 0, 1, 2, 3]


def reuse_distance(bufs):
    n = len(bufs)
    return [next(d for d in range(1, n + 1) if bufs[(c - d) % n] == bufs[c]) for c in range(n)]


def decay_moe_kernel(nc, x, weight, bias, decay_value, gate_w, w1, w2, w3, out):
    B, S, D = x.shape
    T = B * S
    E, _, M = w1.shape
    NT = T // P
    DC = D // P
    MC = M // len(RAW_BUF)
    NCH = M // MC
    MP = MC // P
    SLOTS = TPS * P
    NS = (TOP_K * T + E * (SLOTS - 1)) // SLOTS
    NST = NS + 1
    NTAB = NST * TPS
    G = 4
    NG = NT // G
    NKT = TOP_K * NT
    PICK = 8
    MAX_SB = -(-T // SLOTS)
    W13 = DC * 2 * MC
    W2E = MP * D
    RAW_DIST, W2_DIST = map(reuse_distance, (RAW_BUF, W2_BUF))

    def w2_used(k):
        q, r = divmod(k, NCH)
        return q * (NCH - 1) + r + 1 if r < NCH - 1 else (q + 1) * (NCH - 1) + 1

    RAW_CREDIT = 1 + max(RAW_DIST[n % NCH] - n - 1 for n in range(2, NCH + 2))
    USED_CREDIT = 1 + max(-w2_used(n - W2_DIST[n % NCH]) for n in range(1, NCH + 1))
    DECAY_CREDIT = 2
    XN_CREDIT = 16
    BASE_CREDIT = 4
    G_CREDIT = 2
    GT_CREDIT = 1
    Y_CREDIT = 1

    xf = x.rearrange("b s d -> (b s) d")
    x_tiles = xf.rearrange("(g q p) d -> g p q d", p=P, q=G)
    out_tiles = out[0:T, :].rearrange("(g q p) d -> g p q d", p=P, q=G)
    xn_dram = nc.dram_tensor("xn_rows", (T + P, D), F32).ap()
    xn_tiles = xn_dram[0:T, :].rearrange("(t p) d -> t p d", p=P)

    ctx = ExitStack()
    with ctx:
        ctx.enter_context(nc.allow_non_contiguous_dma(reason="small vectors"))
        at = [nc.sbuf_base + (-nc.sbuf_base) % 64]

        def place(name, shape, dt, offset=None):
            size = 4
            for n in shape[1:]:
                size *= n
            if offset is None:
                offset = at[0]
                at[0] += size + (-size) % 64
            return nc.alloc_sbuf_tensor_at(name, shape, dt, offset=offset)

        raw_at, raw = [], []
        for b in range(3):
            raw_at.append(at[0])
            raw.append(place(f"w_raw{b}", [P, W13 + W2E], F32))
        w13_at, w13_hi, w13_lo = [], [], []
        for b in range(4):
            w13_at.append(at[0])
            w13_hi.append(place(f"w13_hi{b}", [P, W13], F32R))
            w13_lo.append(place(f"w13_lo{b}", [P, W13], F32R))
        w2_at = []
        w2_hi, w2_lo = [], []
        for b in range(4):
            w2_at.append(at[0])
            w2_hi.append(place(f"w2_hi{b}", [P, W2E], F32R))
            w2_lo.append(place(f"w2_lo{b}", [P, W2E], F32R))
        o = w2_at[1]
        power = [place(f"power{k}", [P, D], F32, o + 4 * D * k) for k in range(2)]
        w1_row = place("w1_row", [P, D], F32, o + 8 * D)
        bias_row = place("bias_row", [P, D], F32, o + 12 * D)
        decay = place("decay", [P, DC, D], F32, o + 16 * D)
        zeros = place("zeros", [P, D], F32, o + (16 + 4 * DC) * D)
        diagonal = place("diagonal", [P, D], F32, o + (20 + 4 * DC) * D)
        ones_row = place("ones_row", [P, D], F32, o + (24 + 4 * DC) * D)
        assert (28 + 4 * DC) * D <= at[0] - o
        x_at = at[0]
        xs = place("xs", [P, NT, D], F32)
        o = x_at
        silu, g, gT_hi, gT_lo, y = [], [], [], [], []
        for j in range(3):
            silu.append(place(f"silu{j}", [P, MC], F32, o)); o += 4 * MC
        for j in range(TPS):
            g.append(place(f"g{j}", [P, MC], F32, o)); o += 4 * MC
        for j in range(TPS):
            gT_hi.append(place(f"gT_hi{j}", [P, MP, P], F32R, o)); o += 4 * MC
            gT_lo.append(place(f"gT_lo{j}", [P, MP, P], F32R, o)); o += 4 * MC
        assert o <= x_at + 4 * (NT - G) * D
        o = x_at + 4 * (NT - TPS) * D
        for j in range(TPS):
            y.append(place(f"y{j}", [P, D], F32, o)); o += 4 * D
        xg_at = at[0]
        xg = [place(f"x_rows{j}", [P, D], F32) for j in range(TPS)]
        xT_at = at[0]
        xT_hi = [place(f"xT_hi{j}", [P, DC, P], F32R) for j in range(TPS)]
        xT_lo = [place(f"xT_lo{j}", [P, DC, P], F32R) for j in range(TPS)]
        pick_tile = place("pick_tile", [P, NKT, 2, NTAB], F32, xT_at)
        logitsT = place("logitsT", [P, T], F32, xT_at)
        assert T <= TPS * 2 * D
        xn = [place(f"xn{q}", [P, D], F32, xg_at + 4 * D * q) for q in range(G)]
        assert G <= TPS and NKT * 2 * NTAB <= TPS * 2 * D
        xnT = place("xnT", [P, NT, DC, P], F32, w13_at[2])
        assert NT * D <= 4 * W13
        decay_out = [place(f"decay_out{q}", [P, D], F32, raw_at[2] + 4 * D * q) for q in range(G)]
        assert G * D <= W13 + W2E
        pick_lane = place("pick_lane", [P, NKT, P], F32, w13_at[1])
        assert NKT * P <= 2 * W13

        ident = place("ident", [P, P], F32)
        before = place("before", [P, P], F32)
        ones = place("ones", [P, P], F32)
        lane_iota = place("lane_iota", [P, P], F32)
        scrap = place("scrap", [P, 16], F32)
        token1 = place("token1", [P, NT], F32)
        rev = place("rev", [P, E], F32)
        sb_iota = place("sb_iota", [P, NST], F32)
        spare = place("spare", [P, 1], F32)
        dv = place("dv", [P, 2], F32)
        w0_col = place("w0_col", [P, DC], F32)
        gate = place("gate", [P, DC, E], F32)
        stats = place("stats", [P, NT, 6], F32)
        mv = place("mv", [P, NT, 2], F32)
        eps = place("eps", [P, 1], F32)
        sd = place("sd", [P, NT], F32)
        rs = place("rs", [P, NT], F32)
        nt1 = place("nt1", [P, NT], F32)
        rstd = place("rstd", [P, NT], F32)
        R = [place(f"route{n}", [P, NT, E], F32) for n in range(8)]
        V = [place(f"route_v{n}", [P, NT], F32) for n in range(8)]
        C = [place(f"count{n}", [P, E], F32) for n in range(8)]
        Q = [place(f"sb_tab{n}", [P, NST, E], F32) for n in range(3)]
        slot_f = place("slot_f", [P, TOP_K, NT], F32)
        slot_i = place("slot_i", [P, TOP_K, NT], I32)
        lane_i = place("lane_i", [P, TOP_K, NT], I32)
        tile_i = place("tile_i", [P, TOP_K, NT], I32)
        lane_f = place("lane_f", [P, TOP_K, NT], F32)
        tile_f = place("tile_f", [P, TOP_K, NT], F32)
        top_w = place("top_w", [P, TOP_K, NT], F32)
        tab_f = place("tab_f", [P, 2, NST], F32)
        tab = place("tab", [P, 2, NST], I32)
        slot_w = place("slot_w", [P, NTAB], F32)
        id_f = [place(f"id_f{n}", [P, NTAB], F32) for n in range(3)]
        ids = place("ids", [P, NTAB], U32)
        gather_ids = place("gather_ids", [P, TPS], U32)
        scatter_ids = place("scatter_ids", [P, TPS], U32)
        assert at[0] <= nc.sbuf_usable_end, (at[0], nc.sbuf_usable_end)

        def psum(name):
            return ctx.enter_context(nc.psum_tensor(name, [P, D], F32))

        ab = [psum(f"ab{b}") for b in range(2)]
        gT_ps = psum("gT_ps")
        out_ps = [psum(f"out_ps{j}") for j in range(TPS)]
        decay_ps = [gT_ps, out_ps[TPS - 1]]
        logitsT_ps = [out_ps[1], out_ps[2]]
        logits = out_ps[0][:, 0:NT * E]
        prefix_ps = out_ps[1][:, 0:NT * E]
        total_ps = out_ps[2][:, 0:NT * E]
        table_ps = out_ps[3][:, 0:2 * NTAB]

        def sem(name):
            return ctx.enter_context(nc.semaphore(name))

        x_loaded = [sem(f"x_loaded{n}") for n in range(NG)]
        dv_loaded = sem("dv_loaded")
        w1_loaded = sem("w1_loaded")
        w0_loaded = sem("w0_loaded")
        gate_loaded = sem("gate_loaded")
        bias_loaded = sem("bias_loaded")
        consts_ready = sem("consts_ready")
        dve_step = sem("dve_step")
        decay_ready = sem("decay_ready")
        var_ready = sem("var_ready")
        sd_ready = sem("sd_ready")
        xn_ready = sem("xn_ready")
        xn_stored = [sem(f"xn_stored{q}") for q in range(G)]
        xnT_full = sem("xnT_full")
        xnT_ready = sem("xnT_ready")
        logitsT_full = sem("logitsT_full")
        logitsT_ready = sem("logitsT_ready")
        logits_full = sem("logits_full")
        decay_full = sem("decay_full")
        decay_out_ready = sem("decay_out_ready")
        bias_added = sem("bias_added")
        base_ready = sem("base_ready")
        base_stored = sem("base_stored")
        last_base_stored = sem("last_base_stored")
        spare_stored = sem("spare_stored")
        shifted_ready = sem("shifted_ready")
        exp_ready = sem("exp_ready")
        chosen_ready = sem("chosen_ready")
        prefix_full = sem("prefix_full")
        tab_ready = sem("tab_ready")
        pick_ready = sem("pick_ready")
        table_full = sem("table_full")
        ids_ready = sem("ids_ready")
        raw_loaded = [sem(f"raw_loaded{b}") for b in range(3)]
        hi13_done = sem("hi13_done")
        hi2_done = sem("hi2_done")
        lo13_done = sem("lo13_done")
        lo2_done = sem("lo2_done")
        chunk_used = sem("chunk_used")
        ids_copied = sem("ids_copied")
        gathered = [sem(f"gathered{j}") for j in range(TPS)]
        xT_full = sem("xT_full")
        xT_hi_done = sem("xT_hi_done")
        xT_ready = sem("xT_ready")
        ab_full = sem("ab_full")
        silu_ready = sem("silu_ready")
        g_ready = sem("g_ready")
        gT_full = sem("gT_full")
        gT_hi_done = sem("gT_hi_done")
        gT_ready = sem("gT_ready")
        out_full = sem("out_full")
        y_ready = sem("y_ready")
        y_added = sem("y_added")

        NT_ROW, EXPERT_ROW = 0, 1

        def tiles_of(eng, s):
            return eng.value_load(tab[0:1, NT_ROW, ds(s, 1)], min_val=0, max_val=TPS)

        def expert_of(eng, s):
            return eng.value_load(tab[0:1, EXPERT_ROW, ds(s, 1)], min_val=0, max_val=E - 1)

        def for_tiles(eng, nt, body, between=None):
            for j in reversed(range(TPS)):
                if j:
                    with eng.If(nt > j):
                        body(j)
                else:
                    body(j)
                if between:
                    between(TPS - 1 - j)

        def up_bank(step, j):
            return gT_ps if step == 0 and j == 0 else ab[j % 2]

        def silu_of(step, j):
            return silu[2 if step == 0 and j == 0 else j % 2]

        def bc(ap, shape):
            return ap.to_broadcast(shape)

        block = ctx.enter_context(nc.Block())

        @block.sync
        def _(sp):
            sp.dma_start(dv[:, :], decay_value.rearrange("k a -> a k").to_broadcast([P, 2])).then_inc(dv_loaded, 16)
            sp.dma_start(w1_row[:, :], weight[1:2, :].to_broadcast([P, D])).then_inc(w1_loaded, 16)
            for n in range(NG):
                sp.dma_start(xs[:, n * G:(n + 1) * G, :], x_tiles[n]).then_inc(x_loaded[n], 16)
                if n == 0:
                    sp.dma_start(w0_col[:, :], weight[0, :].rearrange("(k p) -> p k", p=P)).then_inc(w0_loaded, 16)
                    sp.dma_start(gate[:, :, :], gate_w.rearrange("(k p) e -> p k e", p=P)).then_inc(gate_loaded, 16)
                    sp.dma_start(bias_row[:, :], bias.rearrange("(a d) -> a d", a=1).to_broadcast([P, D]))\
                        .then_inc(bias_loaded, 16)
            with sp.Fori(0, NG) as i:
                for q in range(G):
                    sp.wait_ge(xn_ready, i * G + q + 1)
                    sp.dma_start(xn_tiles[ds(i * G + q, 1)].rearrange("a p d -> (a p) d"),
                                 xn[q][:, :]).then_inc(xn_stored[q], 16)
            sp.wait_ge(tab_ready, 1)

            def load_chunk(expert, c, buf):
                w13_dst = raw[buf][:, 0:W13].rearrange("p (k h m) -> p k h m", k=DC, h=2)
                for h, w in enumerate((w1, w3)):
                    src = w[ds(expert, 1), :, c * MC:(c + 1) * MC].rearrange("a (k p) m -> (a p) k m", p=P)
                    sp.dma_start(w13_dst[:, :, h, :], src).then_inc(raw_loaded[buf], 16)
                src = w2[ds(expert, 1), c * MC:(c + 1) * MC, :].rearrange("a (k p) d -> (a p) k d", p=P)
                sp.dma_start(raw[buf][:, W13:W13 + W2E].rearrange("p (k d) -> p k d", k=MP), src)\
                    .then_inc(raw_loaded[buf], 16)

            expert = expert_of(sp, 0)
            for n in range(2):
                load_chunk(expert, n, RAW_BUF[n])
            sp.wait_ge(base_ready, NT + BASE_CREDIT)
            with sp.Fori(0, NS) as s:
                with sp.If(tiles_of(sp, s) > 0):
                    expert = expert_of(sp, s)
                    for n in range(2, NCH + 2):
                        c = n % NCH
                        sp.wait_ge(lo13_done, s * NCH + (n + 1 - RAW_DIST[c] + RAW_CREDIT))
                        sp.wait_ge(lo2_done, s * NCH + (n + 1 - RAW_DIST[c] + RAW_CREDIT))
                        if n == NCH:
                            expert = expert_of(sp, s + 1)
                        load_chunk(expert, c, RAW_BUF[c])

        @block.gpsimd
        def _(pool):
            pool.memset(zeros[:, :], 0.0).then_inc(consts_ready, 1)
            pool.memset(ones_row[:, :], 1.0).then_inc(consts_ready, 1)
            pool.memset(ones[:, :], 1.0).then_inc(consts_ready, 1)
            pool.iota(lane_iota[:, :], pattern=[[1, P]], base=0, channel_multiplier=0,
                      allow_small_or_imprecise_dtypes=True).then_inc(consts_ready, 1)
            pool.iota(token1[:, :], pattern=[[P, NT]], base=1, channel_multiplier=1,
                      allow_small_or_imprecise_dtypes=True).then_inc(consts_ready, 1)
            pool.iota(rev[:, :], pattern=[[-1, E]], base=E, channel_multiplier=0,
                      allow_small_or_imprecise_dtypes=True).then_inc(consts_ready, 1)
            pool.iota(sb_iota[:, :], pattern=[[1, NST]], base=0, channel_multiplier=0,
                      allow_small_or_imprecise_dtypes=True).then_inc(consts_ready, 1)
            pool.iota(spare[:, :], pattern=[[0, 1]], base=T, channel_multiplier=1,
                      allow_small_or_imprecise_dtypes=True).then_inc(consts_ready, 1)
            pool.memset(eps[:, :], EPS).then_inc(consts_ready, 1)
            pool.wait_ge(consts_ready, 9)
            pool.affine_select(out=diagonal[:, :], in_=ones_row[:, :], compare_op=ALU.is_equal, fill=0.0, base=0,
                               pattern=[[-1, D]], channel_multiplier=1).then_inc(consts_ready, 1)
            pool.affine_select(out=ident[:, :], in_=ones[:, :], compare_op=ALU.is_equal, fill=0.0, base=0,
                               pattern=[[-1, P]], channel_multiplier=1).then_inc(consts_ready, 1)
            pool.affine_select(out=before[:, :], in_=ones[:, :], compare_op=ALU.is_gt, fill=0.0, base=0,
                               pattern=[[1, P]], channel_multiplier=-1).then_inc(consts_ready, 1)
            pool.memset(scrap[:, 0:1], 0.0).then_inc(chunk_used, USED_CREDIT)
            pool.memset(scrap[:, 1:2], 0.0).then_inc(lo2_done, RAW_CREDIT)
            pool.memset(scrap[:, 2:4], 0.0).then_inc(y_ready, Y_CREDIT)
            pool.memset(scrap[:, 5:6], 0.0).then_inc(base_ready, BASE_CREDIT)
            pool.dma_start(xn_dram[T:T + P, :], zeros[:, :]).then_inc(spare_stored, 16)
            pool.dma_start(out[T:T + P, :], zeros[:, :]).then_inc(spare_stored, 16)
            pool.wait_ge(bias_loaded, 16)
            with pool.Fori(0, NG) as i:
                for q in range(G):
                    pool.wait_ge(xn_ready, i * G + q + 1)
                    xt = xs[:, ds(i * G + q, 1), :].rearrange("p a d -> p (a d)")
                    pool.tensor_tensor(xt, xt, bias_row[:, :], ALU.add).then_inc(bias_added, 1)
            pool.wait_ge(bias_added, NT)

            def base_group(i, *stored):
                for q in range(G):
                    pool.wait_ge(decay_out_ready, i * G + (q + 1 + DECAY_CREDIT))
                    xt = xs[:, ds(i * G + q, 1), :].rearrange("p a d -> p (a d)")
                    pool.tensor_tensor(xt, xt, decay_out[q][:, :], ALU.add).then_inc(base_ready, 1)
                pool.wait_ge(base_ready, i * G + (G + BASE_CREDIT))
                pool.dma_start(out_tiles[ds(i, 1)].rearrange("a p q d -> (a p) q d"),
                               xs[:, ds(i * G, G), :]).then_inc(*stored)

            with pool.Fori(0, NG - 1) as i:
                base_group(i, base_stored, 16)

            def lo2(c, s, n):
                pool.wait_ge(hi2_done, s * NCH + (n + 1))
                pool.tensor_tensor(w2_lo[W2_BUF[c]][:, :], raw[RAW_BUF[c]][:, W13:W13 + W2E],
                                   w2_hi[W2_BUF[c]][:, :].bitcast(F32), ALU.subtract).then_inc(lo2_done, 1)

            def gather(s):
                pool.tensor_copy(gather_ids[:, :], ids[:, ds(s * TPS, TPS)]).then_inc(ids_copied, 1)
                pool.reg_add(copies, copies, 1)
                for j in reversed(range(TPS)):
                    pool.wait_ge(spare_stored, 32)
                    pool.wait_ge(ids_copied, copies)
                    pool.indirect_dma_start(xg[j][:, :], None, xn_dram,
                                            bass.IndirectOffsetOnAxis(ap=gather_ids[:, j:j + 1], axis=0))\
                        .then_inc(gathered[j], 16)

            added = pool.alloc_register("added")
            computed = pool.alloc_register("computed")
            copies = pool.alloc_register("copies")
            for r, start in ((added, 0), (computed, Y_CREDIT), (copies, 0)):
                pool.reg_mov(r, start)
            pool.wait_ge(ids_ready, 1)
            for q in range(G):
                pool.wait_ge(xn_stored[q], 16 * NG + XN_CREDIT)
            gather(0)
            base_group(NG - 1, last_base_stored, 16)
            lo2(0, 0, 0)
            with pool.Fori(0, NS) as s:
                nt = tiles_of(pool, s)
                with pool.If(nt > 0):
                    for n in range(1, NCH + 1):
                        lo2(n % NCH, s, n)
                        if n == 2:
                            pool.wait_ge(xT_full, s * TPS + TPS)
                            gather(s + 1)
                        if n == 1:
                            with pool.If(s > 0):
                                pool.wait_ge(y_added, added)
                            pool.tensor_copy(scatter_ids[:, :], ids[:, ds(s * TPS, TPS)]).then_inc(ids_copied, 1)
                            pool.reg_add(copies, copies, 1)
                            pool.wait_ge(ids_copied, copies)

                    def add(j):
                        pool.reg_add(computed, computed, 1)
                        pool.reg_add(added, added, 16)
                        pool.wait_ge(spare_stored, 32)
                        pool.wait_ge(y_ready, computed)
                        pool.indirect_dma_start(out, bass.IndirectOffsetOnAxis(ap=scatter_ids[:, j:j + 1], axis=0),
                                                y[j][:, :], None, compute_op=ALU.add).then_inc(y_added, 16)

                    for_tiles(pool, nt, add)
            pool.wait_ge(y_added, added)

        @block.scalar
        def _(act):
            act.wait_ge(consts_ready, 12)

            def turned_out(t, q):
                act.wait_ge(xnT_full, t + 1)
                act.activation(xnT[:, ds(t, 1), :, :].rearrange("p a k t -> p (a k t)"), ab[q % 2][:, :], ACT.Copy)\
                    .then_inc(xnT_ready, 1)

            def root(n):
                act.wait_ge(var_ready, n + 1)
                act.activation(sd[:, n * G:(n + 1) * G], mv[:, n * G:(n + 1) * G, 1], ACT.Sqrt,
                               bias=eps[:, 0:1]).then_inc(sd_ready, 1)

            act.activation(scrap[:, 7:8], eps[:, 0:1], ACT.Sqrt)
            root(0)
            for n in range(NG):
                for q in range(G):
                    turned_out(n * G + q, q)
                if n + 1 < NG:
                    root(n + 1)
                else:
                    act.wait_ge(base_ready, 1)
                    act.activation(scrap[:, 6:7], scrap[:, 5:6], ACT.Exp)
                act.wait_ge(logitsT_full, n + 1)
                act.activation(logitsT[0:E, n * G * P:(n + 1) * G * P], logitsT_ps[n % 2][0:E, :], ACT.Copy)\
                    .then_inc(logitsT_ready, 1)
            act.wait_ge(shifted_ready, 1)
            act.activation(R[1][:, :, :], R[0][:, :, :], ACT.Exp).then_inc(exp_ready, 1)
            act.wait_ge(y_ready, Y_CREDIT)
            act.activation(scrap[:, 4:5], scrap[:, 3:4], ACT.Silu)

            def decayed_out(i, q):
                act.wait_ge(decay_full, i * G + q + 1)
                act.wait_ge(base_ready, i * G + (q + 1 - G + BASE_CREDIT))
                act.activation(decay_out[q][:, :], decay_ps[q % 2][:, :], ACT.Copy).then_inc(decay_out_ready, 1)

            with act.Fori(0, NG - 1) as i:
                for q in range(G):
                    decayed_out(i, q)

            def hi13(s, n, h):
                c = n % NCH
                b = RAW_BUF[c]
                loads = sum(RAW_BUF[m % NCH] == b for m in range(n + 1))
                act.wait_ge(raw_loaded[b], s * (48 * RAW_BUF.count(b)) + 48 * loads)
                part = slice(h * W13 // 2, (h + 1) * W13 // 2)
                act.activation(w13_hi[W13_BUF[c]][:, part], raw[b][:, part], ACT.Copy).then_inc(hi13_done, 1)

            def hi2(s, n):
                c = n % NCH
                if n:
                    act.wait_ge(chunk_used, s * (NCH - 1) + (w2_used(n - W2_DIST[c]) + USED_CREDIT))
                act.activation(w2_hi[W2_BUF[c]][:, :], raw[RAW_BUF[c]][:, W13:W13 + W2E], ACT.Copy)\
                    .then_inc(hi2_done, 1)

            def turn_hi(s, n):
                j = TPS - 1 - n
                act.wait_ge(xT_full, s * TPS + (n + 1))
                act.activation(xT_hi[j][:, :, :].rearrange("p k t -> p (k t)"), ab[j % 2][:, :], ACT.Copy)\
                    .then_inc(xT_hi_done, 1)

            for h in range(2):
                hi13(0, 0, h)
            hi2(0, 0)
            act.wait_ge(table_full, 1)
            for h in range(2):
                hi13(0, 1, h)
            for q in range(G):
                decayed_out(NG - 1, q)
            for n in range(TPS):
                turn_hi(0, n)
            act.wait_ge(base_stored, 16 * (NG - 1))
            units = act.alloc_register("act_units")
            turned = act.alloc_register("act_turned")
            tiles = act.alloc_register("act_tiles")
            for r in (units, turned, tiles):
                act.reg_mov(r, 0)
            with act.Fori(0, NS) as s:
                nt = tiles_of(act, s)
                with act.If(nt > 0):
                    for step in range(NCH + 1):
                        def gate(j):
                            act.reg_add(units, units, 1)
                            act.wait_ge(ab_full, units)
                            act.activation(silu_of(step, j)[:, :], up_bank(step, j)[:, 0:MC], ACT.Silu)\
                                .then_inc(silu_ready, 1)

                        def split_g(j):
                            act.reg_add(turned, turned, 1)
                            act.wait_ge(gT_full, turned)
                            act.activation(gT_hi[j][:, :, :].rearrange("p k t -> p (k t)"),
                                           gT_ps[:, 0:MC], ACT.Copy).then_inc(gT_hi_done, 1)

                        def unit(j):
                            if step == 1:
                                gate(j)
                            if step > 0:
                                split_g(j)
                            if step != 1 and step < NCH:
                                gate(j)

                        def split(place):
                            if step == NCH:
                                turn_hi(s + 1, place)
                            elif place == TPS - 1:
                                for h in range(2):
                                    hi13(s, step + 2, h)
                                hi2(s, step + 1)

                        for_tiles(act, nt, unit, split)

                    def result(j):
                        act.reg_add(tiles, tiles, 1)
                        act.wait_ge(out_full, tiles)
                        act.wait_ge(last_base_stored, 16)
                        act.wait_ge(ids_copied, s * 2 + 2)
                        act.activation(y[j][:, :], out_ps[j][:, :], ACT.Copy,
                                       scale=slot_w[:, ds(s * TPS + j, 1)]).then_inc(y_ready, 1)

                    for_tiles(act, nt, result)

        @block.vector
        def _(dve):
            steps = [0]

            def step_of(ins):
                steps[0] += 1
                ins.then_inc(dve_step, 1)
                return steps[0]

            def chain(ins):
                dve.wait_ge(dve_step, step_of(ins))

            dve.memset(scrap[:, 8:9], 0.0).then_inc(decay_out_ready, DECAY_CREDIT)
            dve.memset(scrap[:, 9:10], 0.0).then_inc(lo13_done, RAW_CREDIT)
            dve.memset(scrap[:, 10:11], 0.0).then_inc(g_ready, G_CREDIT)
            dve.memset(scrap[:, 11:12], 0.0).then_inc(gT_ready, GT_CREDIT)
            for q in range(G):
                dve.memset(scrap[:, 12 + q:13 + q], 0.0).then_inc(xn_stored[q], XN_CREDIT)
            dve.wait_ge(dv_loaded, 16)
            chain(dve.tensor_scalar(dv[:, :], dv[:, :], 0.9, 1.0, ALU.max, ALU.min))
            dve.wait_ge(consts_ready, 12)
            for k in range(2):
                last = dve.tensor_tensor_scan(power[k][:, :], bc(dv[:, k:k + 1], [P, D]), diagonal[:, :], 0.0,
                                              ALU.mult, ALU.add)
            chain(last)
            dve.wait_ge(w1_loaded, 16)
            for k in range(DC):
                n = D - k * P
                last = dve.tensor_tensor(decay[:, k, 0:n], power[1][:, 0:n], w1_row[:, k * P:D], ALU.mult)
            chain(last)

            def variances(n):
                dve.wait_ge(x_loaded[n], 16)
                tiles = range(n * G, (n + 1) * G)
                done = [step_of(dve.bn_stats(stats[:, t, :], xs[:, t, :])) for t in tiles]
                for t, count in zip(tiles, done):
                    dve.wait_ge(dve_step, count)
                    last = dve.bn_aggr(mv[:, t, :], stats[:, t, :])
                last.then_inc(var_ready, 1)

            def normalize(n):
                part = slice(n * G, (n + 1) * G)
                dve.wait_ge(var_ready, n + 1)
                dve.wait_ge(sd_ready, n + 1)
                chain(dve.reciprocal(rs[:, part], sd[:, part]))
                chain(dve.scalar_tensor_tensor(nt1[:, part], mv[:, part, 1], EPS, rs[:, part], ALU.add, ALU.mult))
                chain(dve.scalar_tensor_tensor(nt1[:, part], nt1[:, part], -0.5, rs[:, part], ALU.mult, ALU.mult))
                chain(dve.scalar_tensor_tensor(rstd[:, part], nt1[:, part], 1.5, rs[:, part], ALU.add, ALU.mult))
                for q in range(G):
                    t = n * G + q
                    if n:
                        dve.wait_ge(xnT_full, t - G + 1)
                        dve.wait_ge(xn_stored[q], n * 16 + XN_CREDIT)
                    dve.tensor_scalar(xn[q][:, :], xs[:, t, :], mv[:, t, 0:1], rstd[:, t:t + 1],
                                      ALU.subtract, ALU.mult).then_inc(xn_ready, 1)

            variances(0)
            normalize(0)
            for n in range(1, NG):
                variances(n)
                normalize(n)
            dve.wait_ge(w0_loaded, 16)
            for k in range(DC):
                n = D - k * P
                dve.scalar_tensor_tensor(decay[:, k, 0:n], power[0][:, 0:n], w0_col[:, k:k + 1],
                                         decay[:, k, 0:n], ALU.mult, ALU.add).then_inc(decay_ready, 1)

            te = [P, NT, E]

            def over_e(v):
                return bc(v[:, :].unsqueeze(2), te)

            def by_e(v):
                return bc(v[:, :].unsqueeze(1), te)

            dve.wait_ge(logits_full, NG)
            lg = logits.rearrange("p (t e) -> p t e", e=E)
            chain(dve.tensor_reduce(V[0][:, :], lg, AX_X, ALU.max))
            dve.tensor_tensor(R[0][:, :, :], lg, over_e(V[0]), ALU.subtract).then_inc(shifted_ready, 1)
            dve.wait_ge(exp_ready, 1)
            chain(dve.tensor_reduce(V[1][:, :], R[1][:, :, :], AX_X, ALU.add))
            chain(dve.reciprocal(V[2][:, :], V[1][:, :]))
            chain(dve.tensor_tensor(R[2][:, :, :], R[1][:, :, :], over_e(V[2]), ALU.mult))
            for k, (p, hot) in enumerate(((2, 4), (5, 6))):
                chain(dve.tensor_reduce(V[3 + k][:, :], R[p][:, :, :], AX_X, ALU.max))
                chain(dve.tensor_tensor(R[3][:, :, :], R[p][:, :, :], over_e(V[3 + k]), ALU.is_equal))
                chain(dve.tensor_tensor(R[3][:, :, :], R[3][:, :, :], by_e(rev), ALU.mult))
                chain(dve.tensor_reduce(V[5][:, :], R[3][:, :, :], AX_X, ALU.max))
                chain(dve.tensor_tensor(R[hot][:, :, :], by_e(rev), over_e(V[5]), ALU.is_equal))
                if k == 0:
                    chain(dve.scalar_tensor_tensor(R[5][:, :, :], R[4][:, :, :], -2.0, R[2][:, :, :],
                                                   ALU.mult, ALU.add))
            dve.tensor_tensor(R[7][:, :, :], R[4][:, :, :], R[6][:, :, :], ALU.add).then_inc(chosen_ready, 1)
            chain(dve.tensor_tensor(V[5][:, :], V[3][:, :], V[4][:, :], ALU.add))
            chain(dve.reciprocal(V[6][:, :], V[5][:, :]))
            dve.tensor_tensor(top_w[:, 0, :], V[3][:, :], V[6][:, :], ALU.mult)
            chain(dve.tensor_tensor(top_w[:, 1, :], V[4][:, :], V[6][:, :], ALU.mult))

            dve.wait_ge(prefix_full, 1)
            chain(dve.tensor_copy(R[0][:, :, :], total_ps.rearrange("p (t e) -> p t e", e=E)))
            a, b, k = 0, 1, 1
            while k < NT:
                dve.tensor_copy(R[b][:, 0:k, :], R[a][:, 0:k, :])
                chain(dve.tensor_tensor(R[b][:, k:NT, :], R[a][:, k:NT, :], R[a][:, 0:NT - k, :], ALU.add))
                a, b, k = b, a, 2 * k
            upto, rank = R[a], R[b]
            count = C[0]
            chain(dve.tensor_copy(count[:, :], upto[:, NT - 1, :]))
            chain(dve.tensor_tensor(rank[:, :, :], upto[:, :, :], total_ps.rearrange("p (t e) -> p t e", e=E),
                                    ALU.subtract))
            chain(dve.tensor_tensor(rank[:, :, :], rank[:, :, :], prefix_ps.rearrange("p (t e) -> p t e", e=E),
                                    ALU.add))
            chain(dve.tensor_scalar(C[1][:, :], count[:, :], 0.0, None, ALU.is_gt))
            n_sb, other = C[1], C[2]
            for k in range(1, MAX_SB):
                chain(dve.scalar_tensor_tensor(other[:, :], count[:, :], float(k * SLOTS), n_sb[:, :],
                                               ALU.is_gt, ALU.add))
                n_sb, other = other, n_sb
            a, b, k = n_sb, C[3], 1
            spare_c = [C[4], C[5]]
            while k < E:
                dve.tensor_copy(b[:, 0:k], a[:, 0:k])
                chain(dve.tensor_tensor(b[:, k:E], a[:, k:E], a[:, 0:E - k], ALU.add))
                a, b, k = b, spare_c.pop() if spare_c else None, 2 * k
            sb_end = a
            first_sb = C[6]
            chain(dve.tensor_tensor(first_sb[:, :], sb_end[:, :], n_sb[:, :], ALU.subtract))
            first_slot = C[7]
            chain(dve.tensor_scalar(first_slot[:, :], first_sb[:, :], float(SLOTS), None, ALU.mult))

            se = [P, NST, E]
            s_row = bc(sb_iota[:, :].unsqueeze(2), se)
            chain(dve.tensor_tensor(Q[0][:, :, :], s_row, bc(sb_end[:, :].unsqueeze(1), se), ALU.is_ge))
            chain(dve.tensor_reduce(tab_f[:, EXPERT_ROW, :], Q[0][:, :, :], AX_X, ALU.add))
            dve.tensor_scalar(tab_f[:, EXPERT_ROW, :], tab_f[:, EXPERT_ROW, :], float(E - 1), None, ALU.min)
            chain(dve.tensor_tensor(Q[0][:, :, :], s_row, bc(first_sb[:, :].unsqueeze(1), se), ALU.subtract))
            chain(dve.scalar_tensor_tensor(Q[1][:, :, :], Q[0][:, :, :], -float(SLOTS),
                                           bc(count[:, :].unsqueeze(1), se), ALU.mult, ALU.add))
            chain(dve.tensor_scalar(Q[2][:, :, :], Q[1][:, :, :], 0.0, None, ALU.is_gt))
            for k in range(1, TPS):
                chain(dve.scalar_tensor_tensor(Q[2][:, :, :], Q[1][:, :, :], float(k * P), Q[2][:, :, :],
                                               ALU.is_gt, ALU.add))
            chain(dve.scalar_tensor_tensor(Q[1][:, :, :], Q[0][:, :, :], 0.0, Q[2][:, :, :],
                                           ALU.is_ge, ALU.mult))
            chain(dve.tensor_reduce(tab_f[:, NT_ROW, :], Q[1][:, :, :], AX_X, ALU.add))
            dve.tensor_copy(tab[:, :, :], tab_f[:, :, :]).then_inc(tab_ready, 1)

            chain(dve.tensor_tensor(rank[:, :, :], rank[:, :, :], by_e(first_slot), ALU.add))
            for k, hot in enumerate((4, 6)):
                last = step_of(dve.tensor_tensor(R[3 + 2 * k][:, :, :], R[hot][:, :, :], rank[:, :, :], ALU.mult))
            dve.wait_ge(dve_step, last)
            for k in range(TOP_K):
                last = step_of(dve.tensor_reduce(slot_f[:, k, :], R[3 + 2 * k][:, :, :], AX_X, ALU.add))
            dve.wait_ge(dve_step, last)
            chain(dve.tensor_copy(slot_i[:, :, :], slot_f[:, :, :]))
            lanes = P - 1
            dve.tensor_scalar(lane_i[:, :, :], slot_i[:, :, :], lanes, None, ALU.bitwise_and)
            chain(dve.tensor_scalar(tile_i[:, :, :], slot_i[:, :, :], lanes.bit_length(), None,
                                    ALU.logical_shift_right))
            dve.tensor_copy(lane_f[:, :, :], lane_i[:, :, :])
            chain(dve.tensor_copy(tile_f[:, :, :], tile_i[:, :, :]))
            for k in range(TOP_K):
                for t in range(0, NT, PICK):
                    part, kt = slice(t, t + PICK), slice(k * NT + t, k * NT + t + PICK)
                    lane_shape, tile_shape = [P, PICK, P], [P, PICK, NTAB]

                    def along(v):
                        return bc(v.unsqueeze(2), tile_shape)

                    chain(dve.tensor_tensor(pick_tile[:, kt, 0, :], bc(lane_iota[:, 0:NTAB].unsqueeze(1), tile_shape),
                                            along(tile_f[:, k, part]), ALU.is_equal))
                    chain(dve.tensor_tensor(pick_tile[:, kt, 1, :], pick_tile[:, kt, 0, :],
                                            along(top_w[:, k, part]), ALU.mult))
                    dve.tensor_tensor(pick_tile[:, kt, 0, :], pick_tile[:, kt, 0, :],
                                      along(token1[:, part]), ALU.mult)
                    dve.tensor_tensor(pick_lane[:, kt, :], bc(lane_iota[:, :].unsqueeze(1), lane_shape),
                                      bc(lane_f[:, k, part].unsqueeze(2), lane_shape),
                                      ALU.is_equal).then_inc(pick_ready, 1)

            def lo13(c, s, n, h):
                part = slice(h * W13 // 2, (h + 1) * W13 // 2)
                dve.wait_ge(hi13_done, s * (2 * NCH) + (2 * n + h + 1))
                ins = dve.tensor_tensor(w13_lo[W13_BUF[c]][:, part], raw[RAW_BUF[c]][:, part],
                                        w13_hi[W13_BUF[c]][:, part].bitcast(F32), ALU.subtract)
                if h == 1:
                    ins.then_inc(lo13_done, 1)

            dve.wait_ge(table_full, 1)
            id1 = table_ps[:, 0:NTAB]
            dve.tensor_copy(slot_w[:, :], table_ps[:, NTAB:2 * NTAB])
            dve.tensor_scalar(id_f[0][:, :], id1, 0.0, spare[:, 0:1], ALU.is_equal, ALU.mult)
            chain(dve.tensor_scalar(id_f[1][:, :], id1, -1.0, 0.0, ALU.add, ALU.max))
            chain(dve.tensor_tensor(id_f[2][:, :], id_f[0][:, :], id_f[1][:, :], ALU.add))
            dve.tensor_copy(ids[:, :], id_f[2][:, :]).then_inc(ids_ready, 1)
            for n in range(2):
                for h in range(2):
                    lo13(n, 0, n, h)

            def turn_lo(s, n):
                j = TPS - 1 - n
                dve.wait_ge(xT_hi_done, s * TPS + (n + 1))
                dve.tensor_tensor(xT_lo[j][:, :, :].rearrange("p k t -> p (k t)"), ab[j % 2][:, :],
                                  xT_hi[j][:, :, :].rearrange("p k t -> p (k t)").bitcast(F32),
                                  ALU.subtract).then_inc(xT_ready, 1)

            for n in range(TPS):
                turn_lo(0, n)
            units = dve.alloc_register("dve_units")
            turned = dve.alloc_register("dve_turned")
            dve.reg_mov(units, 0)
            dve.reg_mov(turned, 0)
            with dve.Fori(0, NS) as s:
                nt = tiles_of(dve, s)
                with dve.If(nt > 0):
                    for step in range(NCH + 1):
                        def unit(j):
                            if step > 0:
                                dve.reg_add(turned, turned, 1)
                                dve.wait_ge(gT_hi_done, turned)
                                dve.tensor_tensor(gT_lo[j][:, :, :].rearrange("p k t -> p (k t)"),
                                                  gT_ps[:, 0:MC],
                                                  gT_hi[j][:, :, :].rearrange("p k t -> p (k t)").bitcast(F32),
                                                  ALU.subtract).then_inc(gT_ready, 1)
                            if step < NCH:
                                dve.reg_add(units, units, 1)
                                dve.wait_ge(silu_ready, units)
                                dve.tensor_tensor(g[j][:, :], up_bank(step, j)[:, MC:2 * MC],
                                                  silu_of(step, j)[:, :],
                                                  ALU.mult).then_inc(g_ready, 1)

                        def split(place):
                            n = step + 2
                            if step == NCH:
                                turn_lo(s + 1, place)
                            elif place == TPS - 1:
                                for h in range(2):
                                    lo13(n % NCH, s, n, h)

                        for_tiles(dve, nt, unit, split)

        @block.tensor
        def _(pe):
            def turn(dst, src, *done):
                for k in range(DC):
                    last = pe.transpose(dst[:, k * P:(k + 1) * P], src[:, k * P:(k + 1) * P], ident[:, :])
                last.then_inc(*done)

            pe.wait_ge(consts_ready, 12)
            pe.wait_ge(gate_loaded, 16)

            def turn_xn(t):
                pe.wait_ge(xn_ready, t + 1)
                if t >= 2:
                    pe.wait_ge(xnT_ready, t - 1)
                turn(ab[t % 2], xn[t % G], xnT_full, 1)

            def turn_logits(n):
                pe.wait_ge(logitsT_ready, n + 1)
                for t in range(n * G, (n + 1) * G):
                    last = pe.transpose(logits[:, t * E:(t + 1) * E], logitsT[0:E, t * P:(t + 1) * P],
                                        ident[0:E, 0:E])
                last.then_inc(logits_full, 1)

            for n in range(NG):
                for t in range(n * G, (n + 1) * G):
                    turn_xn(t)
                if n >= 1:
                    turn_logits(n - 1)
                pe.wait_ge(xnT_ready, (n + 1) * G)
                for k in range(DC):
                    last = pe.matmul(logitsT_ps[n % 2][0:E, :].rearrange("e (q t) -> e q t", q=G), gate[:, k, :],
                                     xnT[:, n * G:(n + 1) * G, k, :], start=(k == 0), stop=(k == DC - 1))
                last.then_inc(logitsT_full, 1)
            turn_logits(NG - 1)
            pe.wait_ge(decay_ready, DC)

            def decay_product(t):
                pe.wait_ge(decay_out_ready, t - 1 + DECAY_CREDIT)
                for k in range(DC):
                    last = pe.matmul(decay_ps[t % 2][:, k * P:D], xnT[:, t, k, :], decay[:, k, 0:D - k * P],
                                     start=(k == 0), stop=(k == DC - 1), skip_group_check=True)
                last.then_inc(decay_full, 1)

            PREFIX_AT, TABLE_AT = 3, NT - G
            for t in range(PREFIX_AT):
                decay_product(t)
            pe.wait_ge(chosen_ready, 1)
            chosen = R[7][:, :, :].rearrange("p t e -> p (t e)")
            pe.matmul(prefix_ps, before[:, :], chosen, start=True, stop=True)
            pe.matmul(total_ps, ones[:, :], chosen, start=True, stop=True).then_inc(prefix_full, 1)
            for t in range(PREFIX_AT, TABLE_AT):
                decay_product(t)
            for kt in range(NKT):
                pe.wait_ge(pick_ready, kt // PICK + 1)
                last = pe.matmul(table_ps, pick_lane[:, kt, :],
                                 pick_tile[:, kt, :, :].rearrange("p a n -> p (a n)"),
                                 start=(kt == 0), stop=(kt == NKT - 1))
            last.then_inc(table_full, 1)
            for t in range(TABLE_AT, NT):
                decay_product(t)

            def turn_rows(s, n):
                j = TPS - 1 - n
                pe.wait_ge(gathered[j], s * 16 + 16)
                if n >= 2:
                    pe.wait_ge(xT_ready, s * TPS + (n - 1))
                turn(ab[j % 2], xg[j], xT_full, 1)

            for n in range(TPS):
                turn_rows(0, n)
            before_last = pe.alloc_register("before_last")
            all_g = pe.alloc_register("all_g")
            all_gT = pe.alloc_register("all_gT")
            this_gT = pe.alloc_register("this_gT")
            tiles = pe.alloc_register("tiles")
            for r, start in ((before_last, G_CREDIT - 1), (all_g, G_CREDIT), (all_gT, GT_CREDIT),
                             (this_gT, GT_CREDIT + 1), (tiles, Y_CREDIT)):
                pe.reg_mov(r, start)

            def turn_g(j):
                pe.wait_ge(gT_ready, all_gT)
                for k in range(MP):
                    last = pe.transpose(gT_ps[:, k * P:(k + 1) * P], g[j][:, k * P:(k + 1) * P], ident[:, :])
                last.then_inc(gT_full, 1)
                pe.reg_add(all_gT, all_gT, 1)

            def up(c, j):
                w_hi, w_lo = w13_hi[W13_BUF[c]], w13_lo[W13_BUF[c]]
                pe.wait_ge(g_ready, before_last)
                n = 0
                for k in range(DC):
                    part = slice(k * 2 * MC, (k + 1) * 2 * MC)
                    for lhs, rhs in ((xT_hi, w_hi), (xT_hi, w_lo), (xT_lo, w_hi)):
                        last = pe.matmul(up_bank(c, j)[:, :], lhs[j][:, k, :], rhs[:, part],
                                         start=(n == 0), stop=(n == 3 * DC - 1))
                        n += 1
                last.then_inc(ab_full, 1)
                pe.reg_add(before_last, before_last, 1)
                pe.reg_add(all_g, all_g, 1)

            def down(c, j):
                v_hi, v_lo = w2_hi[W2_BUF[c]], w2_lo[W2_BUF[c]]
                pe.wait_ge(gT_ready, this_gT)
                pe.reg_add(this_gT, this_gT, 1)
                n = 0
                for k in range(MP):
                    part = slice(k * D, (k + 1) * D)
                    for lhs, rhs in ((gT_hi, v_hi), (gT_hi, v_lo), (gT_lo, v_hi)):
                        last = pe.matmul(out_ps[j][:, :], lhs[j][:, k, :], rhs[:, part],
                                         start=(c == 0 and n == 0),
                                         stop=(c == NCH - 1 and n == 3 * MP - 1))
                        n += 1
                if c == NCH - 1:
                    last.then_inc(out_full, 1)
                    pe.reg_add(tiles, tiles, 1)
                elif j == 0:
                    last.then_inc(chunk_used, 1)

            with pe.Fori(0, NS) as s:
                nt = tiles_of(pe, s)
                with pe.If(nt > 0):
                    for step in range(NCH):
                        if step != 1:
                            pe.wait_ge(g_ready, all_g)
                        pe.wait_ge(lo13_done, s * NCH + (step + 1 + RAW_CREDIT))
                        if step == 0:
                            pe.wait_ge(xT_ready, s * TPS + TPS)

                        def unit(j):
                            if step > 1:
                                turn_g(j)
                            up(step, j)
                            if step == 1:
                                pe.wait_ge(g_ready, before_last)
                                turn_g(j)

                        for_tiles(pe, nt, unit)
                        if step > 0:
                            pe.wait_ge(lo2_done, s * NCH + (step + RAW_CREDIT))
                            if step == 1:
                                pe.wait_ge(y_ready, tiles)
                            for_tiles(pe, nt, lambda j: down(step - 1, j))
                    pe.wait_ge(g_ready, all_g)
                    pe.wait_ge(lo2_done, s * NCH + (NCH + RAW_CREDIT))

                    def finish(place):
                        turn_rows(s + 1, place)
                        if place:
                            tile = TPS - place
                            with pe.If(nt > tile):
                                down(NCH - 1, tile)

                    for_tiles(pe, nt, turn_g, finish)
                    down(NCH - 1, 0)


_INS = ['L0_attn_x', 'L0_attn_weight', 'L0_attn_bias', 'L0_attn_decay_value', 'L0_ffn_gate_w',
        'L0_ffn_w1', 'L0_ffn_w2', 'L0_ffn_w3']


def kernel(**inputs):
    import numpy as _np
    import concourse.bacc as _bacc
    from concourse import mybir as _mybir
    from concourse.bass_utils import run_bass_kernel_spmd as _run

    nc = _bacc.Bacc("TRN2", target_bir_lowering=False, num_devices=1)
    arrays, args = {}, []
    for name in _INS:
        a = _np.ascontiguousarray(inputs[name])
        arrays[f"in_{name}_dram"] = a
        args.append(nc.dram_tensor(f"in_{name}_dram", a.shape, _mybir.dt.from_np(a.dtype), kind="ExternalInput").ap())
    B, S, D = inputs['L0_attn_x'].shape
    out = nc.dram_tensor("out_0_dram", (B * S + 128, D), _mybir.dt.from_np(_np.dtype('float32')),
                         kind="ExternalOutput").ap()
    decay_moe_kernel(nc, *args, out)
    r = _run(nc, [arrays], core_ids=[0])
    return r.results[0]["out_0_dram"][:B * S].reshape(B, S, D)
```

```python
from contextlib import ExitStack

import concourse.bass as bass
from concourse import mybir

F32 = mybir.dt.float32
F32R = mybir.dt.float32r
I32 = mybir.dt.int32
U32 = mybir.dt.uint32
ALU = mybir.AluOpType
ACT = mybir.ActivationFunctionType
AX_X = mybir.AxisListType.X
ds = bass.ds

P = 128
TOP_K = 2
EPS = 1e-5
TPS = 5
SHORT = 32

SIZES = [(n, n * P) for n in range(1, TPS)] + [(TPS, (TPS - 1) * P + SHORT), (TPS, TPS * P)]

RAW_BUF = [0, 1, 2, 0, 1, 2, 1]
W13_BUF = [0, 1, 2, 0, 1, 2, 3]
W2_BUF = [0, 1, 2, 0, 1, 2, 3]


def reuse_distance(bufs):
    n = len(bufs)
    return [next(d for d in range(1, n + 1) if bufs[(c - d) % n] == bufs[c]) for c in range(n)]


def decay_moe_kernel(nc, x, weight, bias, decay_value, gate_w, w1, w2, w3, out):
    B, S, D = x.shape
    T = B * S
    E, _, M = w1.shape
    NT = T // P
    DC = D // P
    MC = M // len(RAW_BUF)
    NCH = M // MC
    MP = MC // P
    SLOTS = TPS * P
    MOVE = 512
    NS = (TOP_K * T + E * (SLOTS - 1)) // SLOTS
    NST = NS + 1
    NTAB = NST * TPS
    G = 4
    NG = NT // G
    NKT = TOP_K * NT
    PICK = 8
    MAX_SB = -(-T // SLOTS)
    W13 = DC * 2 * MC
    W2E = MP * D
    RAW_DIST, W2_DIST = map(reuse_distance, (RAW_BUF, W2_BUF))

    def w2_used(k):
        q, r = divmod(k, NCH)
        return q * (NCH - 1) + r + 1 if r < NCH - 1 else (q + 1) * (NCH - 1) + 1

    RAW_CREDIT = 1 + max(RAW_DIST[n % NCH] - n - 1 for n in range(2, NCH + 2))
    USED_CREDIT = 1 + max(-w2_used(n - W2_DIST[n % NCH]) for n in range(1, NCH + 1))
    DECAY_CREDIT = 2
    XN_CREDIT = 16
    BASE_CREDIT = 4
    G_CREDIT = 2
    SILU_CREDIT = 1
    Y_CREDIT = 1

    xf = x.rearrange("b s d -> (b s) d")
    x_tiles = xf.rearrange("(g q p) d -> g p q d", p=P, q=G)
    out_tiles = out[0:T, :].rearrange("(g q p) d -> g p q d", p=P, q=G)
    xn_dram = nc.dram_tensor("xn_rows", (T + P, D), F32).ap()
    xn_tiles = xn_dram[0:T, :].rearrange("(t p) d -> t p d", p=P)

    ctx = ExitStack()
    with ctx:
        ctx.enter_context(nc.allow_non_contiguous_dma(reason="small vectors"))
        at = [nc.sbuf_base + (-nc.sbuf_base) % 64]

        def place(name, shape, dt, offset=None):
            size = 4
            for n in shape[1:]:
                size *= n
            if offset is None:
                offset = at[0]
                at[0] += size + (-size) % 64
            return nc.alloc_sbuf_tensor_at(name, shape, dt, offset=offset)

        raw_at, raw = [], []
        for b in range(3):
            raw_at.append(at[0])
            raw.append(place(f"w_raw{b}", [P, W13 + W2E], F32))
        w13_at, w13_hi, w13_lo = [], [], []
        for b in range(4):
            w13_at.append(at[0])
            w13_hi.append(place(f"w13_hi{b}", [P, W13], F32R))
            w13_lo.append(place(f"w13_lo{b}", [P, W13], F32R))
        w2_at = []
        w2_hi, w2_lo = [], []
        for b in range(4):
            w2_at.append(at[0])
            w2_hi.append(place(f"w2_hi{b}", [P, W2E], F32R))
            w2_lo.append(place(f"w2_lo{b}", [P, W2E], F32R))
        o = w2_at[1]
        power = [place(f"power{k}", [P, D], F32, o + 4 * D * k) for k in range(2)]
        w1_row = place("w1_row", [P, D], F32, o + 8 * D)
        bias_row = place("bias_row", [P, D], F32, o + 12 * D)
        decay = place("decay", [P, DC, D], F32, o + 16 * D)
        zeros = place("zeros", [P, D], F32, o + (16 + 4 * DC) * D)
        diagonal = place("diagonal", [P, D], F32, o + (20 + 4 * DC) * D)
        ones_row = place("ones_row", [P, D], F32, o + (24 + 4 * DC) * D)
        assert (28 + 4 * DC) * D <= at[0] - o
        x_at = at[0]
        xs = place("xs", [P, NT, D], F32)
        o = x_at
        silu, g, gT_hi, gT_lo = [], [], [], []
        for b in range(2):
            silu.append(place(f"silu{b}", [P, MOVE], F32, o)); o += 4 * MOVE
            g.append(place(f"g{b}", [P, MOVE], F32, o)); o += 4 * MOVE
        for b in range(2):
            assert b or o + 8 * MP * SLOTS <= x_at + 4 * (NT - G) * D
            gT_hi.append(place(f"gT_hi{b}", [P, MP, SLOTS], F32R, o)); o += 4 * MP * SLOTS
            gT_lo.append(place(f"gT_lo{b}", [P, MP, SLOTS], F32R, o)); o += 4 * MP * SLOTS
        assert o <= x_at + 4 * NT * D
        xg_at = at[0]
        xg = [place(f"x_rows{j}", [P, D], F32) for j in range(TPS)]
        y = xg
        xT_at = at[0]
        xT_hi = place("xT_hi", [P, DC, SLOTS], F32R)
        xT_lo = place("xT_lo", [P, DC, SLOTS], F32R)
        pick_tile = place("pick_tile", [P, NKT, 2, NTAB], F32, xT_at)
        logitsT = place("logitsT", [P, T], F32, xT_at)
        assert T <= TPS * 2 * D
        xn = [place(f"xn{q}", [P, D], F32, xg_at + 4 * D * q) for q in range(G)]
        assert G <= TPS and NKT * 2 * NTAB <= TPS * 2 * D
        xnT = place("xnT", [P, NT, DC, P], F32, w13_at[2])
        assert NT * D <= 4 * W13
        decay_out = [place(f"decay_out{q}", [P, D], F32, raw_at[2] + 4 * D * q) for q in range(G)]
        assert G * D <= W13 + W2E
        pick_lane = place("pick_lane", [P, NKT, P], F32, w13_at[1])
        assert NKT * P <= 2 * W13

        ident = place("ident", [P, P], F32)
        before = place("before", [P, P], F32)
        ones = place("ones", [P, P], F32)
        lane_iota = place("lane_iota", [P, P], F32)
        scrap = place("scrap", [P, 16], F32)
        token1 = place("token1", [P, NT], F32)
        rev = place("rev", [P, E], F32)
        sb_iota = place("sb_iota", [P, NST], F32)
        spare = place("spare", [P, 1], F32)
        dv = place("dv", [P, 2], F32)
        w0_col = place("w0_col", [P, DC], F32)
        gate = place("gate", [P, DC, E], F32)
        stats = place("stats", [P, NT, 6], F32)
        mv = place("mv", [P, NT, 2], F32)
        eps = place("eps", [P, 1], F32)
        sd = place("sd", [P, NT], F32)
        rs = place("rs", [P, NT], F32)
        nt1 = place("nt1", [P, NT], F32)
        rstd = place("rstd", [P, NT], F32)
        R = [place(f"route{n}", [P, NT, E], F32) for n in range(8)]
        V = [place(f"route_v{n}", [P, NT], F32) for n in range(8)]
        C = [place(f"count{n}", [P, E], F32) for n in range(8)]
        Q = [place(f"sb_tab{n}", [P, NST, E], F32) for n in range(3)]
        slot_f = place("slot_f", [P, TOP_K, NT], F32)
        slot_i = place("slot_i", [P, TOP_K, NT], I32)
        lane_i = place("lane_i", [P, TOP_K, NT], I32)
        tile_i = place("tile_i", [P, TOP_K, NT], I32)
        lane_f = place("lane_f", [P, TOP_K, NT], F32)
        tile_f = place("tile_f", [P, TOP_K, NT], F32)
        top_w = place("top_w", [P, TOP_K, NT], F32)
        tab_f = place("tab_f", [P, 2, NST], F32)
        tab = place("tab", [P, 2, NST], I32)
        slot_w = place("slot_w", [P, NTAB], F32)
        id_f = [place(f"id_f{n}", [P, NTAB], F32) for n in range(3)]
        ids = place("ids", [P, NTAB], U32)
        gather_ids = place("gather_ids", [P, TPS], U32)
        scatter_ids = place("scatter_ids", [P, TPS], U32)
        assert at[0] <= nc.sbuf_usable_end, (at[0], nc.sbuf_usable_end)

        def psum(name):
            return ctx.enter_context(nc.psum_tensor(name, [P, D], F32))

        up_ps = [psum(f"up_ps{b}") for b in range(3)]
        ab = up_ps[0:2]
        out_ps = [psum(f"out_ps{j}") for j in range(TPS)]
        decay_ps = [up_ps[2], out_ps[TPS - 1]]
        logitsT_ps = [out_ps[1], out_ps[2]]
        logits = out_ps[0][:, 0:NT * E]
        prefix_ps = out_ps[1][:, 0:NT * E]
        total_ps = out_ps[2][:, 0:NT * E]
        table_ps = out_ps[3][:, 0:2 * NTAB]

        def sem(name):
            return ctx.enter_context(nc.semaphore(name))

        x_loaded = [sem(f"x_loaded{n}") for n in range(NG)]
        dv_loaded = sem("dv_loaded")
        w1_loaded = sem("w1_loaded")
        w0_loaded = sem("w0_loaded")
        gate_loaded = sem("gate_loaded")
        bias_loaded = sem("bias_loaded")
        consts_ready = sem("consts_ready")
        dve_step = sem("dve_step")
        decay_ready = sem("decay_ready")
        var_ready = sem("var_ready")
        sd_ready = sem("sd_ready")
        xn_ready = sem("xn_ready")
        xn_stored = [sem(f"xn_stored{q}") for q in range(G)]
        xnT_full = sem("xnT_full")
        xnT_ready = sem("xnT_ready")
        logitsT_full = sem("logitsT_full")
        logitsT_ready = sem("logitsT_ready")
        logits_full = sem("logits_full")
        decay_full = sem("decay_full")
        decay_out_ready = sem("decay_out_ready")
        bias_added = sem("bias_added")
        base_ready = sem("base_ready")
        base_stored = sem("base_stored")
        last_base_stored = sem("last_base_stored")
        spare_stored = sem("spare_stored")
        shifted_ready = sem("shifted_ready")
        exp_ready = sem("exp_ready")
        chosen_ready = sem("chosen_ready")
        prefix_full = sem("prefix_full")
        tab_ready = sem("tab_ready")
        pick_ready = sem("pick_ready")
        table_full = sem("table_full")
        ids_ready = sem("ids_ready")
        raw_loaded = [sem(f"raw_loaded{b}") for b in range(3)]
        hi13_done = sem("hi13_done")
        hi2_done = sem("hi2_done")
        lo13_done = sem("lo13_done")
        lo2_done = sem("lo2_done")
        chunk_used = sem("chunk_used")
        ids_copied = sem("ids_copied")
        gathered = [sem(f"gathered{j}") for j in range(TPS)]
        xT_full = sem("xT_full")
        xT_hi_done = sem("xT_hi_done")
        xT_ready = sem("xT_ready")
        up_full = sem("up_full")
        silu_ready = sem("silu_ready")
        g_ready = sem("g_ready")
        gT_hi_done = sem("gT_hi_done")
        gT_ready = sem("gT_ready")
        out_full = sem("out_full")
        y_ready = sem("y_ready")
        y_added = sem("y_added")

        SIZE_ROW, EXPERT_ROW = 0, 1

        def size_of(eng, s):
            return eng.value_load(tab[0:1, SIZE_ROW, ds(s, 1)], min_val=0, max_val=len(SIZES))

        def expert_of(eng, s):
            return eng.value_load(tab[0:1, EXPERT_ROW, ds(s, 1)], min_val=0, max_val=E - 1)

        def for_size(eng, size, program):
            for n, (tiles, tokens) in enumerate(SIZES):
                with eng.If(size > n):
                    with eng.If(size < n + 2):
                        program(tiles, tokens)

        def units_of(step, tokens):
            runs = -(-tokens // MOVE)
            n = tokens // runs
            units = [(r * n, n, mb) for r in range(runs) for mb in range(MP)]
            return [(step * len(units) + u, *unit) for u, unit in enumerate(units)]

        def up_bank(product):
            return up_ps[product % 3]

        def turn_bank(tokens, n):
            return up_bank(2 * len(units_of(0, tokens)) * NCH + n if tokens else n)

        def row_tile(ap, j):
            return ap[:, :, j * P:(j + 1) * P]

        def bc(ap, shape):
            return ap.to_broadcast(shape)

        block = ctx.enter_context(nc.Block())

        @block.sync
        def _(sp):
            sp.dma_start(dv[:, :], decay_value.rearrange("k a -> a k").to_broadcast([P, 2])).then_inc(dv_loaded, 16)
            sp.dma_start(w1_row[:, :], weight[1:2, :].to_broadcast([P, D])).then_inc(w1_loaded, 16)
            for n in range(NG):
                sp.dma_start(xs[:, n * G:(n + 1) * G, :], x_tiles[n]).then_inc(x_loaded[n], 16)
                if n == 0:
                    sp.dma_start(w0_col[:, :], weight[0, :].rearrange("(k p) -> p k", p=P)).then_inc(w0_loaded, 16)
                    sp.dma_start(gate[:, :, :], gate_w.rearrange("(k p) e -> p k e", p=P)).then_inc(gate_loaded, 16)
                    sp.dma_start(bias_row[:, :], bias.rearrange("(a d) -> a d", a=1).to_broadcast([P, D]))\
                        .then_inc(bias_loaded, 16)
            with sp.Fori(0, NG) as i:
                for q in range(G):
                    sp.wait_ge(xn_ready, i * G + q + 1)
                    sp.dma_start(xn_tiles[ds(i * G + q, 1)].rearrange("a p d -> (a p) d"),
                                 xn[q][:, :]).then_inc(xn_stored[q], 16)
            sp.wait_ge(tab_ready, 1)

            def load_chunk(expert, c, buf):
                w13_dst = raw[buf][:, 0:W13].rearrange("p (k h m) -> p k h m", k=DC, h=2)
                for h, w in enumerate((w1, w3)):
                    src = w[ds(expert, 1), :, c * MC:(c + 1) * MC].rearrange("a (k p) m -> (a p) k m", p=P)
                    sp.dma_start(w13_dst[:, :, h, :], src).then_inc(raw_loaded[buf], 16)
                src = w2[ds(expert, 1), c * MC:(c + 1) * MC, :].rearrange("a (k p) d -> (a p) k d", p=P)
                sp.dma_start(raw[buf][:, W13:W13 + W2E].rearrange("p (k d) -> p k d", k=MP), src)\
                    .then_inc(raw_loaded[buf], 16)

            expert = expert_of(sp, 0)
            for n in range(2):
                load_chunk(expert, n, RAW_BUF[n])
            sp.wait_ge(base_ready, NT + BASE_CREDIT)
            with sp.Fori(0, NS) as s:
                with sp.If(size_of(sp, s) > 0):
                    expert = expert_of(sp, s)
                    for n in range(2, NCH + 2):
                        c = n % NCH
                        sp.wait_ge(lo13_done, s * NCH + (n + 1 - RAW_DIST[c] + RAW_CREDIT))
                        sp.wait_ge(lo2_done, s * NCH + (n + 1 - RAW_DIST[c] + RAW_CREDIT))
                        if n == NCH:
                            expert = expert_of(sp, s + 1)
                        load_chunk(expert, c, RAW_BUF[c])

        @block.gpsimd
        def _(pool):
            pool.memset(zeros[:, :], 0.0).then_inc(consts_ready, 1)
            pool.memset(ones_row[:, :], 1.0).then_inc(consts_ready, 1)
            pool.memset(ones[:, :], 1.0).then_inc(consts_ready, 1)
            pool.iota(lane_iota[:, :], pattern=[[1, P]], base=0, channel_multiplier=0,
                      allow_small_or_imprecise_dtypes=True).then_inc(consts_ready, 1)
            pool.iota(token1[:, :], pattern=[[P, NT]], base=1, channel_multiplier=1,
                      allow_small_or_imprecise_dtypes=True).then_inc(consts_ready, 1)
            pool.iota(rev[:, :], pattern=[[-1, E]], base=E, channel_multiplier=0,
                      allow_small_or_imprecise_dtypes=True).then_inc(consts_ready, 1)
            pool.iota(sb_iota[:, :], pattern=[[1, NST]], base=0, channel_multiplier=0,
                      allow_small_or_imprecise_dtypes=True).then_inc(consts_ready, 1)
            pool.iota(spare[:, :], pattern=[[0, 1]], base=T, channel_multiplier=1,
                      allow_small_or_imprecise_dtypes=True).then_inc(consts_ready, 1)
            pool.memset(eps[:, :], EPS).then_inc(consts_ready, 1)
            pool.wait_ge(consts_ready, 9)
            pool.affine_select(out=diagonal[:, :], in_=ones_row[:, :], compare_op=ALU.is_equal, fill=0.0, base=0,
                               pattern=[[-1, D]], channel_multiplier=1).then_inc(consts_ready, 1)
            pool.affine_select(out=ident[:, :], in_=ones[:, :], compare_op=ALU.is_equal, fill=0.0, base=0,
                               pattern=[[-1, P]], channel_multiplier=1).then_inc(consts_ready, 1)
            pool.affine_select(out=before[:, :], in_=ones[:, :], compare_op=ALU.is_gt, fill=0.0, base=0,
                               pattern=[[1, P]], channel_multiplier=-1).then_inc(consts_ready, 1)
            pool.memset(scrap[:, 0:1], 0.0).then_inc(chunk_used, USED_CREDIT)
            pool.memset(scrap[:, 1:2], 0.0).then_inc(lo2_done, RAW_CREDIT)
            pool.memset(scrap[:, 2:4], 0.0).then_inc(y_ready, Y_CREDIT)
            pool.memset(scrap[:, 5:6], 0.0).then_inc(base_ready, BASE_CREDIT)
            pool.dma_start(xn_dram[T:T + P, :], zeros[:, :]).then_inc(spare_stored, 16)
            pool.dma_start(out[T:T + P, :], zeros[:, :]).then_inc(spare_stored, 16)
            pool.wait_ge(bias_loaded, 16)
            with pool.Fori(0, NG) as i:
                for q in range(G):
                    pool.wait_ge(xn_ready, i * G + q + 1)
                    xt = xs[:, ds(i * G + q, 1), :].rearrange("p a d -> p (a d)")
                    pool.tensor_tensor(xt, xt, bias_row[:, :], ALU.add).then_inc(bias_added, 1)
            pool.wait_ge(bias_added, NT)

            def base_group(i, *stored):
                for q in range(G):
                    pool.wait_ge(decay_out_ready, i * G + (q + 1 + DECAY_CREDIT))
                    xt = xs[:, ds(i * G + q, 1), :].rearrange("p a d -> p (a d)")
                    pool.tensor_tensor(xt, xt, decay_out[q][:, :], ALU.add).then_inc(base_ready, 1)
                pool.wait_ge(base_ready, i * G + (G + BASE_CREDIT))
                pool.dma_start(out_tiles[ds(i, 1)].rearrange("a p q d -> (a p) q d"),
                               xs[:, ds(i * G, G), :]).then_inc(*stored)

            with pool.Fori(0, NG - 1) as i:
                base_group(i, base_stored, 16)

            def lo2(c, s, n):
                pool.wait_ge(hi2_done, s * NCH + (n + 1))
                pool.tensor_tensor(w2_lo[W2_BUF[c]][:, :], raw[RAW_BUF[c]][:, W13:W13 + W2E],
                                   w2_hi[W2_BUF[c]][:, :].bitcast(F32), ALU.subtract).then_inc(lo2_done, 1)

            def gather(s):
                pool.tensor_copy(gather_ids[:, :], ids[:, ds(s * TPS, TPS)]).then_inc(ids_copied, 1)
                pool.reg_add(copies, copies, 1)
                for j in reversed(range(TPS)):
                    pool.wait_ge(spare_stored, 32)
                    pool.wait_ge(ids_copied, copies)
                    pool.indirect_dma_start(xg[j][:, :], None, xn_dram,
                                            bass.IndirectOffsetOnAxis(ap=gather_ids[:, j:j + 1], axis=0))\
                        .then_inc(gathered[j], 16)

            added = pool.alloc_register("added")
            computed = pool.alloc_register("computed")
            copies = pool.alloc_register("copies")
            for r, start in ((added, 0), (computed, Y_CREDIT), (copies, 0)):
                pool.reg_mov(r, start)
            pool.wait_ge(ids_ready, 1)
            for q in range(G):
                pool.wait_ge(xn_stored[q], 16 * NG + XN_CREDIT)
            gather(0)
            base_group(NG - 1, last_base_stored, 16)
            lo2(0, 0, 0)
            with pool.Fori(0, NS) as s:
                size = size_of(pool, s)
                with pool.If(size > 0):
                    for n in range(1, NCH + 1):
                        lo2(n % NCH, s, n)
                        if n == 2:
                            pool.wait_ge(xT_full, s * TPS + TPS)
                            gather(s + 1)
                        if n == 1:
                            with pool.If(s > 0):
                                pool.wait_ge(y_added, added)
                            pool.tensor_copy(scatter_ids[:, :], ids[:, ds(s * TPS, TPS)]).then_inc(ids_copied, 1)
                            pool.reg_add(copies, copies, 1)
                            pool.wait_ge(ids_copied, copies)

                    def add(j):
                        pool.reg_add(computed, computed, 1)
                        pool.reg_add(added, added, 16)
                        pool.wait_ge(spare_stored, 32)
                        pool.wait_ge(y_ready, computed)
                        pool.indirect_dma_start(out, bass.IndirectOffsetOnAxis(ap=scatter_ids[:, j:j + 1], axis=0),
                                                y[j][:, :], None, compute_op=ALU.add).then_inc(y_added, 16)

                    for j in reversed(range(TPS)):
                        with pool.If(size > j):
                            add(j)
            pool.wait_ge(y_added, added)

        @block.scalar
        def _(act):
            act.wait_ge(consts_ready, 12)

            def turned_out(t, q):
                act.wait_ge(xnT_full, t + 1)
                act.activation(xnT[:, ds(t, 1), :, :].rearrange("p a k t -> p (a k t)"), ab[q % 2][:, :], ACT.Copy)\
                    .then_inc(xnT_ready, 1)

            def root(n):
                act.wait_ge(var_ready, n + 1)
                act.activation(sd[:, n * G:(n + 1) * G], mv[:, n * G:(n + 1) * G, 1], ACT.Sqrt,
                               bias=eps[:, 0:1]).then_inc(sd_ready, 1)

            act.activation(scrap[:, 7:8], eps[:, 0:1], ACT.Sqrt)
            root(0)
            for n in range(NG):
                for q in range(G):
                    turned_out(n * G + q, q)
                if n + 1 < NG:
                    root(n + 1)
                else:
                    act.wait_ge(base_ready, 1)
                    act.activation(scrap[:, 6:7], scrap[:, 5:6], ACT.Exp)
                act.wait_ge(logitsT_full, n + 1)
                act.activation(logitsT[0:E, n * G * P:(n + 1) * G * P], logitsT_ps[n % 2][0:E, :], ACT.Copy)\
                    .then_inc(logitsT_ready, 1)
            act.wait_ge(shifted_ready, 1)
            act.activation(R[1][:, :, :], R[0][:, :, :], ACT.Exp).then_inc(exp_ready, 1)
            act.wait_ge(y_ready, Y_CREDIT)
            act.activation(scrap[:, 4:5], scrap[:, 3:4], ACT.Silu)

            def decayed_out(i, q):
                act.wait_ge(decay_full, i * G + q + 1)
                act.wait_ge(base_ready, i * G + (q + 1 - G + BASE_CREDIT))
                act.activation(decay_out[q][:, :], decay_ps[q % 2][:, :], ACT.Copy).then_inc(decay_out_ready, 1)

            with act.Fori(0, NG - 1) as i:
                for q in range(G):
                    decayed_out(i, q)

            def hi13(s, n, h):
                c = n % NCH
                b = RAW_BUF[c]
                loads = sum(RAW_BUF[m % NCH] == b for m in range(n + 1))
                act.wait_ge(raw_loaded[b], s * (48 * RAW_BUF.count(b)) + 48 * loads)
                part = slice(h * W13 // 2, (h + 1) * W13 // 2)
                act.activation(w13_hi[W13_BUF[c]][:, part], raw[b][:, part], ACT.Copy).then_inc(hi13_done, 1)

            def hi2(s, n):
                c = n % NCH
                if n:
                    act.wait_ge(chunk_used, s * (NCH - 1) + (w2_used(n - W2_DIST[c]) + USED_CREDIT))
                act.activation(w2_hi[W2_BUF[c]][:, :], raw[RAW_BUF[c]][:, W13:W13 + W2E], ACT.Copy)\
                    .then_inc(hi2_done, 1)

            def turn_hi(s, n, tokens):
                j = TPS - 1 - n
                act.wait_ge(xT_full, s * TPS + (n + 1))
                act.activation(row_tile(xT_hi, j), turn_bank(tokens, n)[:, :].rearrange("p (k t) -> p k t", k=DC),
                               ACT.Copy).then_inc(xT_hi_done, 1)

            for h in range(2):
                hi13(0, 0, h)
            hi2(0, 0)
            act.wait_ge(table_full, 1)
            for h in range(2):
                hi13(0, 1, h)
            for q in range(G):
                decayed_out(NG - 1, q)
            for n in range(TPS):
                turn_hi(0, n, 0)
            act.wait_ge(base_stored, 16 * (NG - 1))
            w1_full = act.alloc_register("w1_full")
            this_g = act.alloc_register("act_this_g")
            tiles = act.alloc_register("act_tiles")
            for r, start in ((w1_full, 1), (this_g, G_CREDIT + 1), (tiles, 1)):
                act.reg_mov(r, start)
            with act.Fori(0, NS) as s:
                size = size_of(act, s)

                def superblock(n_tiles, tokens):
                    for step in range(NCH):
                        if step == 1:
                            act.wait_ge(last_base_stored, 16)
                        for u, first, n, mb in units_of(step, tokens):
                            act.wait_ge(up_full, w1_full)
                            act.activation(silu[u % 2][:, 0:n], up_bank(2 * u)[:, 0:n], ACT.Silu)\
                                .then_inc(silu_ready, 1)
                            act.reg_add(w1_full, w1_full, 2)
                            act.wait_ge(g_ready, this_g)
                            act.activation(gT_hi[step % 2][:, mb, first:first + n], g[u % 2][:, 0:n], ACT.Copy)\
                                .then_inc(gT_hi_done, 1)
                            act.reg_add(this_g, this_g, 1)
                        for h in range(2):
                            hi13(s, step + 2, h)
                        hi2(s, step + 1)
                    for n in range(TPS):
                        turn_hi(s + 1, n, tokens)
                    for j in reversed(range(n_tiles)):
                        rows = min(P, tokens - j * P)
                        act.wait_ge(ids_copied, s * 2 + 2)
                        act.wait_ge(out_full, tiles)
                        act.activation(y[j][0:rows, :], out_ps[j][0:rows, :], ACT.Copy,
                                       scale=slot_w[0:rows, ds(s * TPS + j, 1)]).then_inc(y_ready, 1)
                        act.reg_add(tiles, tiles, 1)

                for_size(act, size, superblock)

        @block.vector
        def _(dve):
            steps = [0]

            def step_of(ins):
                steps[0] += 1
                ins.then_inc(dve_step, 1)
                return steps[0]

            def chain(ins):
                dve.wait_ge(dve_step, step_of(ins))

            dve.memset(scrap[:, 8:9], 0.0).then_inc(decay_out_ready, DECAY_CREDIT)
            dve.memset(scrap[:, 9:10], 0.0).then_inc(lo13_done, RAW_CREDIT)
            dve.memset(scrap[:, 10:11], 0.0).then_inc(g_ready, G_CREDIT)
            dve.memset(scrap[:, 11:12], 0.0).then_inc(silu_ready, SILU_CREDIT)
            for q in range(G):
                dve.memset(scrap[:, 12 + q:13 + q], 0.0).then_inc(xn_stored[q], XN_CREDIT)
            dve.wait_ge(dv_loaded, 16)
            chain(dve.tensor_scalar(dv[:, :], dv[:, :], 0.9, 1.0, ALU.max, ALU.min))
            dve.wait_ge(consts_ready, 12)
            for k in range(2):
                last = dve.tensor_tensor_scan(power[k][:, :], bc(dv[:, k:k + 1], [P, D]), diagonal[:, :], 0.0,
                                              ALU.mult, ALU.add)
            chain(last)
            dve.wait_ge(w1_loaded, 16)
            for k in range(DC):
                n = D - k * P
                last = dve.tensor_tensor(decay[:, k, 0:n], power[1][:, 0:n], w1_row[:, k * P:D], ALU.mult)
            chain(last)

            def variances(n):
                dve.wait_ge(x_loaded[n], 16)
                tiles = range(n * G, (n + 1) * G)
                done = [step_of(dve.bn_stats(stats[:, t, :], xs[:, t, :])) for t in tiles]
                for t, count in zip(tiles, done):
                    dve.wait_ge(dve_step, count)
                    last = dve.bn_aggr(mv[:, t, :], stats[:, t, :])
                last.then_inc(var_ready, 1)

            def normalize(n):
                part = slice(n * G, (n + 1) * G)
                dve.wait_ge(var_ready, n + 1)
                dve.wait_ge(sd_ready, n + 1)
                chain(dve.reciprocal(rs[:, part], sd[:, part]))
                chain(dve.scalar_tensor_tensor(nt1[:, part], mv[:, part, 1], EPS, rs[:, part], ALU.add, ALU.mult))
                chain(dve.scalar_tensor_tensor(nt1[:, part], nt1[:, part], -0.5, rs[:, part], ALU.mult, ALU.mult))
                chain(dve.scalar_tensor_tensor(rstd[:, part], nt1[:, part], 1.5, rs[:, part], ALU.add, ALU.mult))
                for q in range(G):
                    t = n * G + q
                    if n:
                        dve.wait_ge(xnT_full, t - G + 1)
                        dve.wait_ge(xn_stored[q], n * 16 + XN_CREDIT)
                    dve.tensor_scalar(xn[q][:, :], xs[:, t, :], mv[:, t, 0:1], rstd[:, t:t + 1],
                                      ALU.subtract, ALU.mult).then_inc(xn_ready, 1)

            variances(0)
            normalize(0)
            for n in range(1, NG):
                variances(n)
                normalize(n)
            dve.wait_ge(w0_loaded, 16)
            for k in range(DC):
                n = D - k * P
                dve.scalar_tensor_tensor(decay[:, k, 0:n], power[0][:, 0:n], w0_col[:, k:k + 1],
                                         decay[:, k, 0:n], ALU.mult, ALU.add).then_inc(decay_ready, 1)

            te = [P, NT, E]

            def over_e(v):
                return bc(v[:, :].unsqueeze(2), te)

            def by_e(v):
                return bc(v[:, :].unsqueeze(1), te)

            dve.wait_ge(logits_full, NG)
            lg = logits.rearrange("p (t e) -> p t e", e=E)
            chain(dve.tensor_reduce(V[0][:, :], lg, AX_X, ALU.max))
            dve.tensor_tensor(R[0][:, :, :], lg, over_e(V[0]), ALU.subtract).then_inc(shifted_ready, 1)
            dve.wait_ge(exp_ready, 1)
            chain(dve.tensor_reduce(V[1][:, :], R[1][:, :, :], AX_X, ALU.add))
            chain(dve.reciprocal(V[2][:, :], V[1][:, :]))
            chain(dve.tensor_tensor(R[2][:, :, :], R[1][:, :, :], over_e(V[2]), ALU.mult))
            for k, (p, hot) in enumerate(((2, 4), (5, 6))):
                chain(dve.tensor_reduce(V[3 + k][:, :], R[p][:, :, :], AX_X, ALU.max))
                chain(dve.tensor_tensor(R[3][:, :, :], R[p][:, :, :], over_e(V[3 + k]), ALU.is_equal))
                chain(dve.tensor_tensor(R[3][:, :, :], R[3][:, :, :], by_e(rev), ALU.mult))
                chain(dve.tensor_reduce(V[5][:, :], R[3][:, :, :], AX_X, ALU.max))
                chain(dve.tensor_tensor(R[hot][:, :, :], by_e(rev), over_e(V[5]), ALU.is_equal))
                if k == 0:
                    chain(dve.scalar_tensor_tensor(R[5][:, :, :], R[4][:, :, :], -2.0, R[2][:, :, :],
                                                   ALU.mult, ALU.add))
            dve.tensor_tensor(R[7][:, :, :], R[4][:, :, :], R[6][:, :, :], ALU.add).then_inc(chosen_ready, 1)
            chain(dve.tensor_tensor(V[5][:, :], V[3][:, :], V[4][:, :], ALU.add))
            chain(dve.reciprocal(V[6][:, :], V[5][:, :]))
            dve.tensor_tensor(top_w[:, 0, :], V[3][:, :], V[6][:, :], ALU.mult)
            chain(dve.tensor_tensor(top_w[:, 1, :], V[4][:, :], V[6][:, :], ALU.mult))

            dve.wait_ge(prefix_full, 1)
            chain(dve.tensor_copy(R[0][:, :, :], total_ps.rearrange("p (t e) -> p t e", e=E)))
            a, b, k = 0, 1, 1
            while k < NT:
                dve.tensor_copy(R[b][:, 0:k, :], R[a][:, 0:k, :])
                chain(dve.tensor_tensor(R[b][:, k:NT, :], R[a][:, k:NT, :], R[a][:, 0:NT - k, :], ALU.add))
                a, b, k = b, a, 2 * k
            upto, rank = R[a], R[b]
            count = C[0]
            chain(dve.tensor_copy(count[:, :], upto[:, NT - 1, :]))
            chain(dve.tensor_tensor(rank[:, :, :], upto[:, :, :], total_ps.rearrange("p (t e) -> p t e", e=E),
                                    ALU.subtract))
            chain(dve.tensor_tensor(rank[:, :, :], rank[:, :, :], prefix_ps.rearrange("p (t e) -> p t e", e=E),
                                    ALU.add))
            chain(dve.tensor_scalar(C[1][:, :], count[:, :], 0.0, None, ALU.is_gt))
            n_sb, other = C[1], C[2]
            for k in range(1, MAX_SB):
                chain(dve.scalar_tensor_tensor(other[:, :], count[:, :], float(k * SLOTS), n_sb[:, :],
                                               ALU.is_gt, ALU.add))
                n_sb, other = other, n_sb
            a, b, k = n_sb, C[3], 1
            spare_c = [C[4], C[5]]
            while k < E:
                dve.tensor_copy(b[:, 0:k], a[:, 0:k])
                chain(dve.tensor_tensor(b[:, k:E], a[:, k:E], a[:, 0:E - k], ALU.add))
                a, b, k = b, spare_c.pop() if spare_c else None, 2 * k
            sb_end = a
            first_sb = C[6]
            chain(dve.tensor_tensor(first_sb[:, :], sb_end[:, :], n_sb[:, :], ALU.subtract))
            first_slot = C[7]
            chain(dve.tensor_scalar(first_slot[:, :], first_sb[:, :], float(SLOTS), None, ALU.mult))

            se = [P, NST, E]
            s_row = bc(sb_iota[:, :].unsqueeze(2), se)
            chain(dve.tensor_tensor(Q[0][:, :, :], s_row, bc(sb_end[:, :].unsqueeze(1), se), ALU.is_ge))
            chain(dve.tensor_reduce(tab_f[:, EXPERT_ROW, :], Q[0][:, :, :], AX_X, ALU.add))
            dve.tensor_scalar(tab_f[:, EXPERT_ROW, :], tab_f[:, EXPERT_ROW, :], float(E - 1), None, ALU.min)
            chain(dve.tensor_tensor(Q[0][:, :, :], s_row, bc(first_sb[:, :].unsqueeze(1), se), ALU.subtract))
            chain(dve.scalar_tensor_tensor(Q[1][:, :, :], Q[0][:, :, :], -float(SLOTS),
                                           bc(count[:, :].unsqueeze(1), se), ALU.mult, ALU.add))
            chain(dve.tensor_scalar(Q[2][:, :, :], Q[1][:, :, :], 0.0, None, ALU.is_gt))
            for _, less in SIZES[:-1]:
                chain(dve.scalar_tensor_tensor(Q[2][:, :, :], Q[1][:, :, :], float(less), Q[2][:, :, :],
                                               ALU.is_gt, ALU.add))
            chain(dve.scalar_tensor_tensor(Q[1][:, :, :], Q[0][:, :, :], 0.0, Q[2][:, :, :],
                                           ALU.is_ge, ALU.mult))
            chain(dve.tensor_reduce(tab_f[:, SIZE_ROW, :], Q[1][:, :, :], AX_X, ALU.add))
            dve.tensor_copy(tab[:, :, :], tab_f[:, :, :]).then_inc(tab_ready, 1)

            chain(dve.tensor_tensor(rank[:, :, :], rank[:, :, :], by_e(first_slot), ALU.add))
            for k, hot in enumerate((4, 6)):
                last = step_of(dve.tensor_tensor(R[3 + 2 * k][:, :, :], R[hot][:, :, :], rank[:, :, :], ALU.mult))
            dve.wait_ge(dve_step, last)
            for k in range(TOP_K):
                last = step_of(dve.tensor_reduce(slot_f[:, k, :], R[3 + 2 * k][:, :, :], AX_X, ALU.add))
            dve.wait_ge(dve_step, last)
            chain(dve.tensor_copy(slot_i[:, :, :], slot_f[:, :, :]))
            lanes = P - 1
            dve.tensor_scalar(lane_i[:, :, :], slot_i[:, :, :], lanes, None, ALU.bitwise_and)
            chain(dve.tensor_scalar(tile_i[:, :, :], slot_i[:, :, :], lanes.bit_length(), None,
                                    ALU.logical_shift_right))
            dve.tensor_copy(lane_f[:, :, :], lane_i[:, :, :])
            chain(dve.tensor_copy(tile_f[:, :, :], tile_i[:, :, :]))
            for k in range(TOP_K):
                for t in range(0, NT, PICK):
                    part, kt = slice(t, t + PICK), slice(k * NT + t, k * NT + t + PICK)
                    lane_shape, tile_shape = [P, PICK, P], [P, PICK, NTAB]

                    def along(v):
                        return bc(v.unsqueeze(2), tile_shape)

                    chain(dve.tensor_tensor(pick_tile[:, kt, 0, :], bc(lane_iota[:, 0:NTAB].unsqueeze(1), tile_shape),
                                            along(tile_f[:, k, part]), ALU.is_equal))
                    chain(dve.tensor_tensor(pick_tile[:, kt, 1, :], pick_tile[:, kt, 0, :],
                                            along(top_w[:, k, part]), ALU.mult))
                    dve.tensor_tensor(pick_tile[:, kt, 0, :], pick_tile[:, kt, 0, :],
                                      along(token1[:, part]), ALU.mult)
                    dve.tensor_tensor(pick_lane[:, kt, :], bc(lane_iota[:, :].unsqueeze(1), lane_shape),
                                      bc(lane_f[:, k, part].unsqueeze(2), lane_shape),
                                      ALU.is_equal).then_inc(pick_ready, 1)

            def lo13(c, s, n, h):
                part = slice(h * W13 // 2, (h + 1) * W13 // 2)
                dve.wait_ge(hi13_done, s * (2 * NCH) + (2 * n + h + 1))
                ins = dve.tensor_tensor(w13_lo[W13_BUF[c]][:, part], raw[RAW_BUF[c]][:, part],
                                        w13_hi[W13_BUF[c]][:, part].bitcast(F32), ALU.subtract)
                if h == 1:
                    ins.then_inc(lo13_done, 1)

            dve.wait_ge(table_full, 1)
            id1 = table_ps[:, 0:NTAB]
            dve.tensor_copy(slot_w[:, :], table_ps[:, NTAB:2 * NTAB])
            dve.tensor_scalar(id_f[0][:, :], id1, 0.0, spare[:, 0:1], ALU.is_equal, ALU.mult)
            chain(dve.tensor_scalar(id_f[1][:, :], id1, -1.0, 0.0, ALU.add, ALU.max))
            chain(dve.tensor_tensor(id_f[2][:, :], id_f[0][:, :], id_f[1][:, :], ALU.add))
            dve.tensor_copy(ids[:, :], id_f[2][:, :]).then_inc(ids_ready, 1)
            for n in range(2):
                for h in range(2):
                    lo13(n, 0, n, h)

            def turn_lo(s, n, tokens):
                j = TPS - 1 - n
                dve.wait_ge(xT_hi_done, s * TPS + (n + 1))
                dve.tensor_tensor(row_tile(xT_lo, j), turn_bank(tokens, n)[:, :].rearrange("p (k t) -> p k t", k=DC),
                                  row_tile(xT_hi, j).bitcast(F32), ALU.subtract).then_inc(xT_ready, 1)

            for n in range(TPS):
                turn_lo(0, n, 0)
            w3_full = dve.alloc_register("w3_full")
            this_silu = dve.alloc_register("this_silu")
            this_hi = dve.alloc_register("this_hi")
            for r, start in ((w3_full, 2), (this_silu, SILU_CREDIT + 1), (this_hi, 1)):
                dve.reg_mov(r, start)
            with dve.Fori(0, NS) as s:
                size = size_of(dve, s)

                def superblock(n_tiles, tokens):
                    for step in range(NCH):
                        for u, first, n, mb in units_of(step, tokens):
                            dve.wait_ge(silu_ready, this_silu)
                            dve.wait_ge(up_full, w3_full)
                            dve.tensor_tensor(g[u % 2][:, 0:n], up_bank(2 * u + 1)[:, 0:n], silu[u % 2][:, 0:n],
                                              ALU.mult).then_inc(g_ready, 1)
                            dve.reg_add(this_silu, this_silu, 1)
                            dve.reg_add(w3_full, w3_full, 2)
                            dve.wait_ge(gT_hi_done, this_hi)
                            run = slice(first, first + n)
                            dve.tensor_tensor(gT_lo[step % 2][:, mb, run], g[u % 2][:, 0:n],
                                              gT_hi[step % 2][:, mb, run].bitcast(F32),
                                              ALU.subtract).then_inc(gT_ready, 1)
                            dve.reg_add(this_hi, this_hi, 1)
                        for h in range(2):
                            lo13((step + 2) % NCH, s, step + 2, h)
                    for n in range(TPS):
                        turn_lo(s + 1, n, tokens)

                for_size(dve, size, superblock)

        @block.tensor
        def _(pe):
            def turn(dst, src, *done):
                for k in range(DC):
                    last = pe.transpose(dst[:, k * P:(k + 1) * P], src[:, k * P:(k + 1) * P], ident[:, :])
                last.then_inc(*done)

            pe.wait_ge(consts_ready, 12)
            pe.wait_ge(gate_loaded, 16)

            def turn_xn(t):
                pe.wait_ge(xn_ready, t + 1)
                if t >= 2:
                    pe.wait_ge(xnT_ready, t - 1)
                turn(ab[t % 2], xn[t % G], xnT_full, 1)

            def turn_logits(n):
                pe.wait_ge(logitsT_ready, n + 1)
                for t in range(n * G, (n + 1) * G):
                    last = pe.transpose(logits[:, t * E:(t + 1) * E], logitsT[0:E, t * P:(t + 1) * P],
                                        ident[0:E, 0:E])
                last.then_inc(logits_full, 1)

            for n in range(NG):
                for t in range(n * G, (n + 1) * G):
                    turn_xn(t)
                if n >= 1:
                    turn_logits(n - 1)
                pe.wait_ge(xnT_ready, (n + 1) * G)
                for k in range(DC):
                    last = pe.matmul(logitsT_ps[n % 2][0:E, :].rearrange("e (q t) -> e q t", q=G), gate[:, k, :],
                                     xnT[:, n * G:(n + 1) * G, k, :], start=(k == 0), stop=(k == DC - 1))
                last.then_inc(logitsT_full, 1)
            turn_logits(NG - 1)
            pe.wait_ge(decay_ready, DC)

            def decay_product(t):
                pe.wait_ge(decay_out_ready, t - 1 + DECAY_CREDIT)
                for k in range(DC):
                    last = pe.matmul(decay_ps[t % 2][:, k * P:D], xnT[:, t, k, :], decay[:, k, 0:D - k * P],
                                     start=(k == 0), stop=(k == DC - 1), skip_group_check=True)
                last.then_inc(decay_full, 1)

            PREFIX_AT, TABLE_AT = 3, NT - G
            for t in range(PREFIX_AT):
                decay_product(t)
            pe.wait_ge(chosen_ready, 1)
            chosen = R[7][:, :, :].rearrange("p t e -> p (t e)")
            pe.matmul(prefix_ps, before[:, :], chosen, start=True, stop=True)
            pe.matmul(total_ps, ones[:, :], chosen, start=True, stop=True).then_inc(prefix_full, 1)
            for t in range(PREFIX_AT, TABLE_AT):
                decay_product(t)
            for kt in range(NKT):
                pe.wait_ge(pick_ready, kt // PICK + 1)
                last = pe.matmul(table_ps, pick_lane[:, kt, :],
                                 pick_tile[:, kt, :, :].rearrange("p a n -> p (a n)"),
                                 start=(kt == 0), stop=(kt == NKT - 1))
            last.then_inc(table_full, 1)
            for t in range(TABLE_AT, NT):
                decay_product(t)

            for n in range(TPS):
                pe.wait_ge(gathered[TPS - 1 - n], 16)
                if n == 2:
                    pe.wait_ge(decay_out_ready, NT - 1 + DECAY_CREDIT)
                if n >= 3:
                    pe.wait_ge(xT_ready, n - 2)
                turn(turn_bank(0, n), xg[TPS - 1 - n], xT_full, 1)
            bank_free = pe.alloc_register("bank_free")
            all_g = pe.alloc_register("all_g")
            chunk_gT = pe.alloc_register("chunk_gT")
            tiles = pe.alloc_register("tiles")
            assert G_CREDIT - 1 == SILU_CREDIT == 1
            for r, start in ((bank_free, SILU_CREDIT), (all_g, G_CREDIT), (chunk_gT, 0), (tiles, Y_CREDIT)):
                pe.reg_mov(r, start)

            def up(c, u, first, n, mb):
                w_hi, w_lo = w13_hi[W13_BUF[c]], w13_lo[W13_BUF[c]]
                for h in range(2):
                    pe.wait_ge(silu_ready if h else g_ready, bank_free)
                    bank = up_bank(2 * u + h)
                    i = 0
                    for k in range(DC):
                        block = slice((2 * k + h) * MC + mb * P, (2 * k + h) * MC + (mb + 1) * P)
                        for lhs, rhs in ((w_hi, xT_hi), (w_hi, xT_lo), (w_lo, xT_hi)):
                            last = pe.matmul(bank[:, 0:n], lhs[:, block], rhs[:, k, first:first + n],
                                             start=(i == 0), stop=(i == 3 * DC - 1))
                            i += 1
                    last.then_inc(up_full, 1)
                pe.reg_add(bank_free, bank_free, 1)
                pe.reg_add(all_g, all_g, 1)

            def down(c, n_tiles, tokens, n_units):
                v_hi, v_lo = w2_hi[W2_BUF[c]], w2_lo[W2_BUF[c]]
                h_hi, h_lo = gT_hi[c % 2], gT_lo[c % 2]
                pe.reg_add(chunk_gT, chunk_gT, n_units)
                pe.wait_ge(gT_ready, chunk_gT)
                for j in reversed(range(n_tiles)):
                    rows = min(P, tokens - j * P)
                    i = 0
                    for k in range(MP):
                        part = slice(k * D, (k + 1) * D)
                        for lhs, rhs in ((h_hi, v_hi), (h_hi, v_lo), (h_lo, v_hi)):
                            last = pe.matmul(out_ps[j][0:rows, :], lhs[:, k, j * P:j * P + rows], rhs[:, part],
                                             start=(c == 0 and i == 0),
                                             stop=(c == NCH - 1 and i == 3 * MP - 1))
                            i += 1
                    if c == NCH - 1:
                        last.then_inc(out_full, 1)
                if c == NCH - 1:
                    pe.reg_add(tiles, tiles, n_tiles)
                else:
                    last.then_inc(chunk_used, 1)

            with pe.Fori(0, NS) as s:
                size = size_of(pe, s)

                def superblock(n_tiles, tokens):
                    n_units = len(units_of(0, tokens))
                    for step in range(NCH):
                        pe.wait_ge(lo13_done, s * NCH + (step + 1 + RAW_CREDIT))
                        if step == 0:
                            pe.wait_ge(xT_ready, s * TPS + TPS)
                        for unit in units_of(step, tokens):
                            up(step, *unit)
                        if step > 0:
                            pe.wait_ge(lo2_done, s * NCH + (step + RAW_CREDIT))
                            if step == 1:
                                pe.wait_ge(y_ready, tiles)
                            down(step - 1, n_tiles, tokens, n_units)
                    for n in range(TPS):
                        pe.wait_ge(gathered[TPS - 1 - n], s * 16 + 32)
                        if n == 0:
                            pe.wait_ge(g_ready, bank_free)
                        elif n == 1:
                            pe.wait_ge(silu_ready, bank_free)
                        elif n == 2:
                            pe.wait_ge(g_ready, all_g)
                        else:
                            pe.wait_ge(xT_ready, s * TPS + (TPS + n - 2))
                        turn(turn_bank(tokens, n), xg[TPS - 1 - n], xT_full, 1)
                    pe.wait_ge(lo2_done, s * NCH + (NCH + RAW_CREDIT))
                    down(NCH - 1, n_tiles, tokens, n_units)

                for_size(pe, size, superblock)


_INS = ['L0_attn_x', 'L0_attn_weight', 'L0_attn_bias', 'L0_attn_decay_value', 'L0_ffn_gate_w',
        'L0_ffn_w1', 'L0_ffn_w2', 'L0_ffn_w3']


def kernel(**inputs):
    import numpy as _np
    import concourse.bacc as _bacc
    from concourse import mybir as _mybir
    from concourse.bass_utils import run_bass_kernel_spmd as _run

    nc = _bacc.Bacc("TRN2", target_bir_lowering=False, num_devices=1)
    arrays, args = {}, []
    for name in _INS:
        a = _np.ascontiguousarray(inputs[name])
        arrays[f"in_{name}_dram"] = a
        args.append(nc.dram_tensor(f"in_{name}_dram", a.shape, _mybir.dt.from_np(a.dtype), kind="ExternalInput").ap())
    B, S, D = inputs['L0_attn_x'].shape
    out = nc.dram_tensor("out_0_dram", (B * S + 128, D), _mybir.dt.from_np(_np.dtype('float32')),
                         kind="ExternalOutput").ap()
    decay_moe_kernel(nc, *args, out)
    r = _run(nc, [arrays], core_ids=[0])
    return r.results[0]["out_0_dram"][:B * S].reshape(B, S, D)
```
